# Optimizing a Trainium2 kernel written in Bass

```python
import numpy as np
import jax
import jax.numpy as jnp

def _softmax(x, axis=-1):
    return jax.nn.softmax(x, axis=axis)

def _gelu(x):
    return jax.nn.gelu(x, approximate=True)

def _silu(x):
    return jax.nn.silu(x)

def _sigmoid(x):
    return jax.nn.sigmoid(x)

def _layernorm(x, axis=-1, eps=1e-05):
    m = jnp.mean(x, axis=axis, keepdims=True)
    v = jnp.var(x, axis=axis, keepdims=True)
    return (x - m) / jnp.sqrt(v + eps)

def _scatter_add(tgt, idx, src, axis=0):
    return tgt.at[idx].add(src)

def _segment_sum(src, seg, n):
    return jax.ops.segment_sum(src, seg, n)
kernel_name = 'mk_xattn_seq_d1_seqx_r8_309422'

def setup_inputs(seed: int=0):
    np.random.seed(seed)
    _w = jnp.asarray

    def _rec_inputs():
        import jax
        import jax.numpy as jnp
        _rk = jax.random.key(seed)
        x = -0.0005207 + 1.001 * jax.random.normal(jax.random.fold_in(_rk, 1), (2, 512, 128), jnp.float32)
        _lenS = 512 - jax.random.randint(jax.random.fold_in(_rk, 7), (2,), 0, max(1, 512 // 4) + 1, jnp.int32)
        _lenS2 = 154 - jax.random.randint(jax.random.fold_in(_rk, 8), (2,), 0, max(1, 154 // 4) + 1, jnp.int32)
        _ctx_1024P = jax.random.normal(jax.random.fold_in(_rk, 11), (2, 16, 128), jnp.float32)
        _ctx_1024c = jax.random.dirichlet(jax.random.fold_in(_rk, 511), 0.3 * jnp.ones((16,), jnp.float32), (2, 154))
        _ctx_1024t = jnp.einsum('bsk,bkd->bsd', _ctx_1024c, _ctx_1024P)
        _ctx_1024t = _ctx_1024t * jax.lax.rsqrt(jnp.mean(jnp.square(_ctx_1024t)) + 1e-12) * 0.953939
        ctx_1024 = 4.13588e-05 + 0.999923 * (_ctx_1024t + 0.3 * jax.random.normal(jax.random.fold_in(_rk, 611), (2, 154, 128), jnp.float32))
        return (x, ctx_1024)
    x, ctx_1024 = _rec_inputs()

    def _L0_xattn_setup():
        import jax, jax.numpy as jnp
        import numpy as np
        D, H, E, K, DFF = (128, 16, 8, 2, 512)
        B, L, T = (4, 64, 256)
        EPS = 1e-05

        def _xavier(key, shape):
            fan_in, fan_out = (shape[-1], shape[-2])
            a = jnp.sqrt(6.0 / (fan_in + fan_out))
            return jax.random.uniform(key, shape, jnp.float32, -a, a)

        def _ln(x, g, b):
            m = x.mean(-1, keepdims=True)
            v = ((x - m) ** 2).mean(-1, keepdims=True)
            return (x - m) / jnp.sqrt(v + EPS) * g + b

        def _mha(q_in, kv_in, in_w, in_b, out_w, out_b):
            wq, wk, wv = jnp.split(in_w, 3, axis=0)
            bq, bk, bv = jnp.split(in_b, 3, axis=0)
            dh = D // H

            def heads(x, w, b):
                y = x @ w.T + b
                return y.reshape(x.shape[0], x.shape[1], H, dh).transpose(0, 2, 1, 3)
            q = heads(q_in, wq, bq)
            k = heads(kv_in, wk, bk)
            v = heads(kv_in, wv, bv)
            scores = jnp.einsum('bhqd,bhkd->bhqk', q, k) / jnp.sqrt(jnp.float32(dh))
            attn = jax.nn.softmax(scores, axis=-1)
            out = jnp.einsum('bhqk,bhkd->bhqd', attn, v)
            out = out.transpose(0, 2, 1, 3).reshape(q_in.shape[0], q_in.shape[1], D)
            return out @ out_w.T + out_b

        def _fuse_moe(x, ln_g, ln_b, rw, rb, fc1_w, fc1_b, fc2_w, fc2_b):
            h = _ln(x, ln_g, ln_b)
            logits = h @ rw.T + rb
            vals, idx = jax.lax.top_k(logits, K)
            gates = jax.nn.softmax(vals, axis=-1)
            N = x.shape[0] * x.shape[1]
            hf = h.reshape(N, D)
            h1 = jax.nn.gelu(jnp.einsum('nd,efd->enf', hf, fc1_w) + fc1_b[:, None, :], approximate=False)
            eo = jnp.einsum('enf,edf->end', h1, fc2_w) + fc2_b[:, None, :]
            idx_f = idx.reshape(N, K)
            gates_f = gates.reshape(N, K)
            gathered = eo[idx_f, jnp.arange(N)[:, None], :]
            mixed = (gathered * gates_f[..., None]).sum(axis=1).reshape(x.shape)
            return x + mixed
        key = jax.random.key(seed)
        ks = jax.random.split(key, 16)
        inp = {'latents': jax.random.normal(ks[0], (B, L, D), jnp.float32), 'tokens': jax.random.normal(ks[1], (B, T, D), jnp.float32), 'sa_ln_g': jnp.ones((D,)), 'sa_ln_b': jnp.zeros((D,)), 'sa_in_w': _xavier(ks[2], (3 * D, D)), 'sa_in_b': jnp.zeros((3 * D,)), 'sa_out_w': _xavier(ks[3], (D, D)), 'sa_out_b': jnp.zeros((D,)), 'ca_q_ln_g': jnp.ones((D,)), 'ca_q_ln_b': jnp.zeros((D,)), 'ca_kv_ln_g': jnp.ones((D,)), 'ca_kv_ln_b': jnp.zeros((D,)), 'ca_in_w': _xavier(ks[4], (3 * D, D)), 'ca_in_b': jnp.zeros((3 * D,)), 'ca_out_w': _xavier(ks[5], (D, D)), 'ca_out_b': jnp.zeros((D,)), 'moe_ln_g': jnp.ones((D,)), 'moe_ln_b': jnp.zeros((D,)), 'router_w': _xavier(ks[6], (E, D)), 'router_b': jnp.zeros((E,)), 'e_fc1_w': jax.vmap(lambda k: _xavier(k, (DFF, D)))(jax.random.split(ks[7], E)), 'e_fc1_b': jnp.zeros((E, DFF)), 'e_fc2_w': jax.vmap(lambda k: _xavier(k, (D, DFF)))(jax.random.split(ks[8], E)), 'e_fc2_b': jnp.zeros((E, D))}
        return inp
    _L0_xattn_all = _L0_xattn_setup()
    _L0_xattn_in = {k: v for k, v in _L0_xattn_all.items() if k in ('sa_ln_g', 'sa_ln_b', 'sa_in_w', 'sa_in_b', 'sa_out_w', 'sa_out_b', 'ca_q_ln_g', 'ca_q_ln_b', 'ca_kv_ln_g', 'ca_kv_ln_b', 'ca_in_w', 'ca_in_b', 'ca_out_w', 'ca_out_b', 'moe_ln_g', 'moe_ln_b', 'router_w', 'router_b', 'e_fc1_w', 'e_fc1_b', 'e_fc2_w', 'e_fc2_b')}
    del _L0_xattn_all
    return {'x': x, 'ctx_1024': ctx_1024, 'L0_xattn_sa_ln_g': _L0_xattn_in['sa_ln_g'], 'L0_xattn_sa_ln_b': _L0_xattn_in['sa_ln_b'], 'L0_xattn_sa_in_w': _L0_xattn_in['sa_in_w'], 'L0_xattn_sa_in_b': _L0_xattn_in['sa_in_b'], 'L0_xattn_sa_out_w': _L0_xattn_in['sa_out_w'], 'L0_xattn_sa_out_b': _L0_xattn_in['sa_out_b'], 'L0_xattn_ca_q_ln_g': _L0_xattn_in['ca_q_ln_g'], 'L0_xattn_ca_q_ln_b': _L0_xattn_in['ca_q_ln_b'], 'L0_xattn_ca_kv_ln_g': _L0_xattn_in['ca_kv_ln_g'], 'L0_xattn_ca_kv_ln_b': _L0_xattn_in['ca_kv_ln_b'], 'L0_xattn_ca_in_w': _L0_xattn_in['ca_in_w'], 'L0_xattn_ca_in_b': _L0_xattn_in['ca_in_b'], 'L0_xattn_ca_out_w': _L0_xattn_in['ca_out_w'], 'L0_xattn_ca_out_b': _L0_xattn_in['ca_out_b'], 'L0_xattn_moe_ln_g': _L0_xattn_in['moe_ln_g'], 'L0_xattn_moe_ln_b': _L0_xattn_in['moe_ln_b'], 'L0_xattn_router_w': _L0_xattn_in['router_w'], 'L0_xattn_router_b': _L0_xattn_in['router_b'], 'L0_xattn_e_fc1_w': _L0_xattn_in['e_fc1_w'], 'L0_xattn_e_fc1_b': _L0_xattn_in['e_fc1_b'], 'L0_xattn_e_fc2_w': _L0_xattn_in['e_fc2_w'], 'L0_xattn_e_fc2_b': _L0_xattn_in['e_fc2_b']}

def reference(x, ctx_1024, L0_xattn_sa_ln_g, L0_xattn_sa_ln_b, L0_xattn_sa_in_w, L0_xattn_sa_in_b, L0_xattn_sa_out_w, L0_xattn_sa_out_b, L0_xattn_ca_q_ln_g, L0_xattn_ca_q_ln_b, L0_xattn_ca_kv_ln_g, L0_xattn_ca_kv_ln_b, L0_xattn_ca_in_w, L0_xattn_ca_in_b, L0_xattn_ca_out_w, L0_xattn_ca_out_b, L0_xattn_moe_ln_g, L0_xattn_moe_ln_b, L0_xattn_router_w, L0_xattn_router_b, L0_xattn_e_fc1_w, L0_xattn_e_fc1_b, L0_xattn_e_fc2_w, L0_xattn_e_fc2_b):
    import jax
    import jax.numpy as jnp

    def _L0_xattn_ref(latents, tokens, sa_ln_g, sa_ln_b, sa_in_w, sa_in_b, sa_out_w, sa_out_b, ca_q_ln_g, ca_q_ln_b, ca_kv_ln_g, ca_kv_ln_b, ca_in_w, ca_in_b, ca_out_w, ca_out_b, moe_ln_g, moe_ln_b, router_w, router_b, e_fc1_w, e_fc1_b, e_fc2_w, e_fc2_b):
        import jax, jax.numpy as jnp
        import numpy as np
        D, H, E, K, DFF = (128, 16, 8, 2, 512)
        B, L, T = (4, 64, 256)
        EPS = 1e-05

        def _xavier(key, shape):
            fan_in, fan_out = (shape[-1], shape[-2])
            a = jnp.sqrt(6.0 / (fan_in + fan_out))
            return jax.random.uniform(key, shape, jnp.float32, -a, a)

        def _ln(x, g, b):
            m = x.mean(-1, keepdims=True)
            v = ((x - m) ** 2).mean(-1, keepdims=True)
            return (x - m) / jnp.sqrt(v + EPS) * g + b

        def _mha(q_in, kv_in, in_w, in_b, out_w, out_b):
            wq, wk, wv = jnp.split(in_w, 3, axis=0)
            bq, bk, bv = jnp.split(in_b, 3, axis=0)
            dh = D // H

            def heads(x, w, b):
                y = x @ w.T + b
                return y.reshape(x.shape[0], x.shape[1], H, dh).transpose(0, 2, 1, 3)
            q = heads(q_in, wq, bq)
            k = heads(kv_in, wk, bk)
            v = heads(kv_in, wv, bv)
            scores = jnp.einsum('bhqd,bhkd->bhqk', q, k) / jnp.sqrt(jnp.float32(dh))
            attn = jax.nn.softmax(scores, axis=-1)
            out = jnp.einsum('bhqk,bhkd->bhqd', attn, v)
            out = out.transpose(0, 2, 1, 3).reshape(q_in.shape[0], q_in.shape[1], D)
            return out @ out_w.T + out_b

        def _fuse_moe(x, ln_g, ln_b, rw, rb, fc1_w, fc1_b, fc2_w, fc2_b):
            h = _ln(x, ln_g, ln_b)
            logits = h @ rw.T + rb
            vals, idx = jax.lax.top_k(logits, K)
            gates = jax.nn.softmax(vals, axis=-1)
            N = x.shape[0] * x.shape[1]
            hf = h.reshape(N, D)
            h1 = jax.nn.gelu(jnp.einsum('nd,efd->enf', hf, fc1_w) + fc1_b[:, None, :], approximate=False)
            eo = jnp.einsum('enf,edf->end', h1, fc2_w) + fc2_b[:, None, :]
            idx_f = idx.reshape(N, K)
            gates_f = gates.reshape(N, K)
            gathered = eo[idx_f, jnp.arange(N)[:, None], :]
            mixed = (gathered * gates_f[..., None]).sum(axis=1).reshape(x.shape)
            return x + mixed
        q = _ln(latents, sa_ln_g, sa_ln_b)
        x = latents + _mha(q, q, sa_in_w, sa_in_b, sa_out_w, sa_out_b)
        qc = _ln(x, ca_q_ln_g, ca_q_ln_b)
        kv = _ln(tokens, ca_kv_ln_g, ca_kv_ln_b)
        x = x + _mha(qc, kv, ca_in_w, ca_in_b, ca_out_w, ca_out_b)
        return _fuse_moe(x, moe_ln_g, moe_ln_b, router_w, router_b, e_fc1_w, e_fc1_b, e_fc2_w, e_fc2_b)
    x = _L0_xattn_ref(x, ctx_1024, L0_xattn_sa_ln_g, L0_xattn_sa_ln_b, L0_xattn_sa_in_w, L0_xattn_sa_in_b, L0_xattn_sa_out_w, L0_xattn_sa_out_b, L0_xattn_ca_q_ln_g, L0_xattn_ca_q_ln_b, L0_xattn_ca_kv_ln_g, L0_xattn_ca_kv_ln_b, L0_xattn_ca_in_w, L0_xattn_ca_in_b, L0_xattn_ca_out_w, L0_xattn_ca_out_b, L0_xattn_moe_ln_g, L0_xattn_moe_ln_b, L0_xattn_router_w, L0_xattn_router_b, L0_xattn_e_fc1_w, L0_xattn_e_fc1_b, L0_xattn_e_fc2_w, L0_xattn_e_fc2_b)
    return x

_drawn_inputs = setup_inputs


def setup_inputs(seed=0):
    import zlib

    import numpy as np

    out = dict(_drawn_inputs(seed))
    spreads = {'L0_xattn_sa_ln_g': (1.0, 0.2),
     'L0_xattn_sa_ln_b': (0.0, 0.1),
     'L0_xattn_sa_in_b': (0.0, 0.1),
     'L0_xattn_sa_out_b': (0.0, 0.1),
     'L0_xattn_ca_q_ln_g': (1.0, 0.2),
     'L0_xattn_ca_q_ln_b': (0.0, 0.334),
     'L0_xattn_ca_kv_ln_g': (1.0, 0.2),
     'L0_xattn_ca_kv_ln_b': (0.0, 0.1),
     'L0_xattn_ca_in_b': (0.0, 0.1),
     'L0_xattn_ca_out_b': (0.0, 0.1),
     'L0_xattn_moe_ln_g': (1.0, 0.2),
     'L0_xattn_moe_ln_b': (0.0, 0.1),
     'L0_xattn_router_b': (0.0, 0.1),
     'L0_xattn_e_fc1_b': (0.0, 0.1),
     'L0_xattn_e_fc2_b': (0.0, 0.1)}
    factors = {}
    for name, (base, spread) in spreads.items():
        noise = np.random.default_rng([zlib.crc32(name.encode()), seed]).standard_normal(out[name].shape)
        drawn = base * np.exp(spread * noise) if base else spread * noise
        out[name] = jnp.asarray(drawn.astype(out[name].dtype))
    for name, factor in factors.items():
        out[name] = (out[name] * factor).astype(out[name].dtype)
    return out
```

```python
from contextlib import ExitStack

import concourse.bass as bass
from concourse import mybir

F32 = mybir.dt.float32
BF16 = mybir.dt.bfloat16
ALU = mybir.AluOpType
ACT = mybir.ActivationFunctionType
AX = mybir.AxisListType

P = 128
B, S, D = 2, 512, 128
T = 154
H, DH = 16, 8
E, FF = 8, 512
EPS = 1e-5
QT = S // P
FC = FF // P
TB = T - P
TP = 160
G = H // 4
SCALE = float(DH) ** -0.5

Q_PARTS = (0, 0, 1, 1, 0, 2)
K_PARTS = (0, 1, 0, 1, 2, 0)
SELF_MAX_ROW = DH * len(Q_PARTS)
CROSS_MAX_ROW = SELF_MAX_ROW + 3

(C_SA_G, C_SA_B, C_CQ_G, C_CQ_B, C_KV_G, C_KV_B, C_MO_G, C_MO_B,
 C_SA_BQ, C_SA_BK, C_SA_BV, C_CA_BQ, C_CA_BK, C_CA_BV) = range(14)
C_FC1_B = 14
C_ROUTER = C_FC1_B + E * FC
N_COLS = C_ROUTER + E
R_SA_OUT, R_CA_OUT, R_ROUTER = 0, D, 2 * D
N_ROWS = 2 * D + E

SELF_UNITS = B * H * 2
LEAD = 12
SELF_MAX = B * H * QT
CROSS_MAX = B * G * 8


def make_plan():
    plan = []
    add = plan.append

    def qkv(p, b):
        return [("hT", p), ("q", p), ("k", b), ("v", b)]

    plan.extend([("ln", 0), ("hat", 0)])
    plan.extend(qkv(0, 0))
    at = {}
    def put(u, *steps):
        at.setdefault(u, []).extend(steps)
    put(0, ("ln", 1))
    put(1, ("hat", 1))
    put(2, ("hT", 1), ("ctx_ln",))
    put(3, ("q", 1))
    put(5, ("k", 1))
    put(7, ("v", 1), ("ctx_hat",))
    put(9, ("ctx_T",))
    put(12, ("ctx_k",))
    put(14, ("ctx_vA",))
    put(17, ("ctx_vB",))

    def finish(u, p):
        put(u, ("osT", p))
        put(u + 2, ("proj", p))
        put(u + 3, ("ln", p + 2))
        put(u + 4, ("hat", p + 2))
        put(u + 5, ("hT", p + 2))
        put(u + 6, ("q", p + 2))
    finish(39, 0)

    for n in range(2 * LEAD):
        add(("max", n))
        if n % 16 == 15:
            add(("mT", n // 16))
    for u in range(SELF_UNITS):
        for n in (2 * (u + LEAD), 2 * (u + LEAD) + 1):
            if n < SELF_MAX:
                add(("max", n))
        add(("scores", u))
        if u % 8 == 4 and (u + LEAD) // 8 <= SELF_MAX // 16 and 8 < u + LEAD:
            g = (u + LEAD) // 8 - 1
            if g >= 1:
                add(("mT", g))
        if u % 4 == 3 and u >= 7:
            add(("pv", u // 4 - 1))
        if u % 8 == 5 and u >= 13:
            add(("oT", u // 8 - 1))
        plan.extend(at.get(u, []))
    def cross_max(c, part):
        if c < B * G:
            for i in range(4 * part, 4 * part + 4):
                add(("max", SELF_MAX + 8 * c + i))
    cross_max(0, 0)
    cross_max(0, 1)
    add(("pv", 15))
    add(("mT", 8))
    cross_max(1, 0)
    cross_max(1, 1)
    add(("oT", 7))
    between = {0: [[("osT", 1)], [("proj", 1)], [("ln", 3)]],
               1: [[("hat", 3), ("hT", 3)], [("q", 3)], []],
               5: [[("osT", 2)], [("proj", 2)], [("ln", 4)]],
               6: [[("hat", 4), ("hT", 4)], [("router", 0)], [("gates", 0)]],
               7: [[("gT", 0)], [("b2", 0)], []]}
    for c in range(B * G):
        extra = between.get(c, [[], [], []])
        if c + 1 < B * G:
            add(("mT", 8 + c + 1))
        if c >= 2:
            add(("oT", 8 + c - 2))
        cross_max(c + 2, 0)
        add(("scores", SELF_UNITS + 3 * c))
        plan.extend(extra[0])
        cross_max(c + 2, 1)
        add(("scores", SELF_UNITS + 3 * c + 1))
        plan.extend(extra[1])
        add(("scores", SELF_UNITS + 3 * c + 2))
        if c >= 1:
            add(("pv", 16 + c - 1))
        plan.extend(extra[2])
    add(("oT", 8 + 6))
    add(("pv", 16 + 7))
    between = {0: [("oT", 15)], 1: [("osT", 3), ("proj", 3)], 2: [("ln", 5)], 3: [("hat", 5), ("hT", 5)],
               4: [("router", 1), ("gates", 1)], 5: [("gT", 1)], 6: [("b2", 1)]}
    for n in range(B * E):
        add(("fc1", n))
        plan.extend(between.get(n, []))
        if n:
            add(("fc2", n - 1))
        if n == E:
            add(("store", 0))
    add(("fc2", B * E - 1))
    add(("store", 1))
    return plan


PLAN = make_plan()
MISC_KINDS = ("hT", "q", "k", "v", "ctx_T", "ctx_k", "ctx_vA", "ctx_vB", "mT", "oT", "osT", "proj", "router", "gT", "b2")
MISC_USE = {step: n for n, step in enumerate(s for s in PLAN if s[0] in MISC_KINDS)}
UNITS = SELF_UNITS + 3 * B * G


def ring_slot(w):
    return w % 8 if w < SELF_UNITS else (4 * ((w - SELF_UNITS) // 3) + (w - SELF_UNITS) % 3) % 8


def quad(w):
    return w // 4 if w < SELF_UNITS else SELF_UNITS // 4 + (w - SELF_UNITS) // 3


def units_until(q):
    return 4 * (q + 1) if q < SELF_UNITS // 4 else SELF_UNITS + 3 * (q - SELF_UNITS // 4 + 1)


def max_until(g):
    return 16 * (g + 1) if g < 8 else SELF_MAX + 8 * (g - 7)


def group_of(w):
    return w // 8 if w < SELF_UNITS else 8 + (w - SELF_UNITS) // 3


def build(nc, x, ctx_in, w_in, w_out, cols, rows, fc1_w, fc2_w, fc2_b, out):
    ctx = ExitStack()
    with ctx:
        def sb(name, shape, dt=F32):
            return ctx.enter_context(nc.sbuf_tensor(name, shape, dt))

        def sem(name):
            return ctx.enter_context(nc.semaphore(name))

        x_sb = sb("x_sb", [P, B, QT, D])
        ctx_sb = sb("ctx_sb", [P, B, 2, D])
        w_in_sb = sb("w_in_sb", [P, 2, 3 * D])
        w_out_sb = sb("w_out_sb", [P, 2, D])
        cols_sb = sb("cols_sb", [P, N_COLS])
        rows_sb = sb("rows_sb", [P, N_ROWS])
        fc2_b_sb = sb("fc2_b_sb", [E, D])
        ident = sb("ident", [P, P])
        ones_row = sb("ones_row", [3, H * S // 4], BF16)
        power = sb("power", [P, QT])
        lower = sb("lower", [P, E, E])
        q_tile = sb("q_tile", [P, B, H, S], BF16)
        k_tile = sb("k_tile", [P, B, H, S], BF16)
        fc1_sb = k_tile[:, 0].bitcast(F32).rearrange("p (e a) n -> p e (a n)", e=E)
        fc2_sb = k_tile[:, 1].bitcast(F32).rearrange("p (e a) n -> p e (a n)", e=E) \
            .rearrange("p e (c d) -> p e c d", c=FC)
        kc_tile = sb("kc_tile", [P, B, H, TP], BF16)
        v_aug = sb("v_aug", [P, B, QT, H, 32])
        vc_aug = sb("vc_aug", [P, B, H, 32])
        vc_diag = sb("vc_diag", [P, B, G, 4, 32])
        probs = sb("probs", [P, 8, 1024])
        q_full, q_rest = sb("q_full", [P, S]), sb("q_rest", [P, S])
        q_part = sb("q_part", [P, 3, S], BF16)
        k_full, k_rest = sb("k_full", [P, S]), sb("k_rest", [P, S])
        k_part = sb("k_part", [P, 3, S], BF16)
        row_max = sb("row_max", [P, 16, 16])
        neg_full, neg_rest = sb("neg_full", [16, 2, P]), sb("neg_rest", [16, 2, P])
        neg_part = sb("neg_part", [16, 2, 3, P], BF16)
        stats = sb("stats", [P, QT, 6])
        mean_var = sb("mean_var", [P, QT, 2])
        rstd = sb("rstd", [P, QT])
        x_hat = sb("x_hat", [P, QT, D])
        c_stats = sb("c_stats", [P, B, 2, 6])
        c_mean_var = sb("c_mean_var", [P, B, 2, 2])
        c_rstd = sb("c_rstd", [P, B, 2])
        var_eps = sb("var_eps", [P, QT])
        c_hat = sb("c_hat", [P, B, 2, D])
        hT = sb("hT", [P, 2, S])
        ctxT = sb("ctxT", [P, B * T])
        o_raw = sb("o_raw", [P, 2, S])
        o_rden = sb("o_rden", [P, QT, 4])
        o_tok = sb("o_tok", [P, 2, QT, H, DH])
        oT = sb("oT", [P, S])
        x_mid = sb("x_mid", [P, B, QT, D])
        x_out = sb("x_out", [P, B, QT, D])
        logit = sb("logit", [P, QT, E])
        beats = sb("beats", [P, E, E])
        ties = sb("ties", [P, E, E])
        rank = sb("rank", [P, QT, E])
        top = sb("top", [P, QT])
        shifted = sb("shifted", [P, QT, E])
        expd = sb("expd", [P, QT, E])
        kept = sb("kept", [P, QT, E])
        gsum = sb("gsum", [P, QT])
        grec = sb("grec", [P, QT])
        gate = sb("gate", [P, B, QT, E])
        gateT = sb("gateT", [E, S])

        ps_s = ctx.enter_context(nc.psum_tensor("ps_s", [P, 4, 512], F32))
        ps_m = ctx.enter_context(nc.psum_tensor("ps_m", [P, 2, 512], F32))
        ps_o = ctx.enter_context(nc.psum_tensor("ps_o", [P, 512], F32))
        ps_x = ctx.enter_context(nc.psum_tensor("ps_x", [P, 512], F32))

        x_loaded = [sem(f"x_loaded{b}") for b in range(B)]
        ctx_loaded, w_in_loaded, w_out_loaded = sem("ctx_loaded"), sem("w_in_loaded"), sem("w_out_loaded")
        cols_loaded, rows_loaded = sem("cols_loaded"), sem("rows_loaded")
        fc1_loaded, fc2_loaded, fc2_b_loaded = sem("fc1_loaded"), sem("fc2_loaded"), sem("fc2_b_loaded")
        ident_ready, ones_ready, lower_ready = sem("ident_ready"), sem("ones_ready"), sem("lower_ready")
        tiles_cleared = [sem(f"tiles_cleared{b}") for b in range(B)]
        ctx_cleared, v_cleared = sem("ctx_cleared"), sem("v_cleared")
        key_ones = [sem(f"key_ones{b}") for b in range(B)]
        ctx_key_ones = sem("ctx_key_ones")
        pool_chain = sem("pool_chain")
        dve_chain = sem("dve_chain")
        misc_filled = sem("misc_filled")
        misc_read = sem("misc_read")
        var_ready = sem("var_ready")
        rstd_ready = sem("rstd_ready")
        hat_ready = sem("hat_ready")
        ctx_hat_ready = sem("ctx_hat_ready")
        hT_ready, ctxT_ready = sem("hT_ready"), sem("ctxT_ready")
        q_high = sem("q_high")
        q_low = sem("q_low")
        k_high, k_low = sem("k_high"), sem("k_low")
        q_moved = [sem(f"q_moved{p}") for p in range(4)]
        k_moved = [sem(f"k_moved{b}") for b in range(B)]
        kc_moved = sem("kc_moved")
        v_ready, vc_ready, vd_ready = sem("v_ready"), sem("vc_ready"), sem("vd_ready")
        max_filled, max_read = sem("max_filled"), sem("max_read")
        neg_high, neg_low = sem("neg_high"), sem("neg_low")
        neg_moved = [sem(f"neg_moved{i}") for i in range(2)]
        scored, exped = sem("scored"), sem("exped")
        pv_done, o_copied = sem("pv_done"), sem("o_copied")
        o_normed, oT_ready, mid_ready = sem("o_normed"), sem("oT_ready"), sem("mid_ready")
        logits_shifted, logits_exped, gates_ready = sem("logits_shifted"), sem("logits_exped"), sem("gates_ready")
        gateT_ready, bias_added = sem("gateT_ready"), sem("bias_added")
        fc1_done, gelu_done = sem("fc1_done"), sem("gelu_done")
        fc2_done, combined = sem("fc2_done"), sem("combined")
        stored = sem("stored")

        norms = {}
        for step in PLAN:
            if step[0] in ("hat", "ctx_hat"):
                norms[step if step[0] == "hat" else "ctx_hat"] = len(norms)

        def phase_input(p):
            return (x_sb, x_mid, x_out)[p // 2][:, p % 2]

        block = ctx.enter_context(nc.Block())

        @block.sync
        def _(sp):
            tokens = x.rearrange("b (t p) d -> b p t d", p=P)
            sp.dma_start(x_sb[:, 0], tokens[0]).then_inc(x_loaded[0], 16)
            sp.dma_start(cols_sb[:, :], cols).then_inc(cols_loaded, 16)
            sp.dma_start(w_in_sb[:, :, :], w_in).then_inc(w_in_loaded, 16)
            sp.dma_start(x_sb[:, 1], tokens[1]).then_inc(x_loaded[1], 16)
            sp.dma_start(ctx_sb[:, :, 0, :], ctx_in[:, 0:P, :].rearrange("b p d -> p b d")).then_inc(ctx_loaded, 16)
            sp.dma_start(ctx_sb[0:TB, :, 1, :], ctx_in[:, P:T, :].rearrange("b p d -> p b d")).then_inc(ctx_loaded, 16)
            sp.dma_start(rows_sb[:, :], rows.partition_broadcast(P)).then_inc(rows_loaded, 16)
            sp.dma_start(w_out_sb[:, :, :], w_out).then_inc(w_out_loaded, 16)
            sp.wait_ge(ones_ready, 1)
            for b in range(B):
                sp.wait_ge(tiles_cleared[b], 2)
                for quarter in range(4):
                    sp.dma_start(k_tile[SELF_MAX_ROW:SELF_MAX_ROW + 3, b, 4 * quarter:4 * quarter + 4, :],
                                 ones_row[:, :]).then_inc(key_ones[b], 16)
                if b == 0:
                    sp.wait_ge(ctx_cleared, 1)
                    for bb in range(B):
                        for half in range(2):
                            sp.dma_start(kc_tile[CROSS_MAX_ROW:CROSS_MAX_ROW + 3, bb, 8 * half:8 * half + 8, :],
                                         ones_row[:, 0:8 * TP]).then_inc(ctx_key_ones, 16)
            sp.dma_start(fc2_b_sb[:, :], fc2_b).then_inc(fc2_b_loaded, 16)
            sp.wait_ge(scored, SELF_UNITS // 2)
            sp.dma_start(fc1_sb, fc1_w).then_inc(fc1_loaded, 16)
            sp.wait_ge(scored, SELF_UNITS)
            sp.dma_start(fc2_sb, fc2_w).then_inc(fc2_loaded, 16)
            for step in PLAN:
                if step[0] == "store":
                    b = step[1]
                    sp.wait_ge(combined, E * (b + 1))
                    sp.dma_start(out[b].rearrange("(t p) d -> p t d", p=P), x_out[:, b]).then_inc(stored, 16)
            sp.wait_ge(stored, 16 * B)

        @block.gpsimd
        def _(pool):
            steps = [0]

            def link(ins):
                steps[0] += 1
                ins.then_inc(pool_chain, 1)
                pool.wait_ge(pool_chain, steps[0])

            link(nc.gpsimd.memset(ident[:, :], 0.0))
            nc.gpsimd.affine_select(out=ident[:, :], in_=ident[:, :], compare_op=ALU.not_equal, fill=1.0, base=0,
                                    pattern=[[-1, P]], channel_multiplier=1).then_inc(ident_ready, 1)
            nc.gpsimd.memset(q_tile[:, 0].bitcast(F32), 0.0).then_inc(tiles_cleared[0], 1)
            link(nc.gpsimd.memset(power[:, :], -0.5))
            nc.gpsimd.memset(ones_row[:, :], 1.0).then_inc(ones_ready, 1)
            for b in range(B):
                nc.gpsimd.memset(v_aug[:, b, :, :, DH + 1:], 0.0).then_inc(v_cleared, 1)
                nc.gpsimd.memset(v_aug[:, b, :, :, DH:DH + 1], 1.0).then_inc(v_cleared, 1)
                if b == 0:
                    nc.gpsimd.memset(q_tile[:, 1].bitcast(F32), 0.0).then_inc(tiles_cleared[1], 1)
            nc.gpsimd.memset(k_tile[:, 1].bitcast(F32), 0.0).then_inc(tiles_cleared[1], 1)
            nc.gpsimd.memset(kc_tile[:, :, :, :], 0.0).then_inc(ctx_cleared, 1)
            nc.gpsimd.memset(vc_aug[:, :, :, DH + 1:], 0.0).then_inc(ctx_cleared, 1)
            nc.gpsimd.memset(vc_aug[:, :, :, DH:DH + 1], 1.0).then_inc(ctx_cleared, 1)
            link(nc.gpsimd.memset(vc_diag[:, :, :, :, :], 0.0))
            for j in range(4):
                nc.gpsimd.memset(vc_diag[32 * j:32 * j + TB, :, :, j, DH:DH + 1], 1.0).then_inc(ctx_cleared, 1)
                pool.wait_ge(ctx_cleared, 4 + j)
            link(nc.gpsimd.memset(lower[:, :, :], 1.0))
            nc.gpsimd.affine_select(out=lower[:, :, :], in_=lower[:, :, :], compare_op=ALU.is_gt, fill=0.0, base=0,
                                    pattern=[[1, E], [-1, E]], channel_multiplier=0).then_inc(lower_ready, 1)

            def k_split(n, width, moved):
                pool.wait_ge(k_high, n + 1)
                if n:
                    pool.wait_ge(*moved)
                link(nc.gpsimd.tensor_tensor(k_rest[:, 0:width], k_full[:, 0:width], k_part[:, 0, 0:width], ALU.subtract))
                link(nc.gpsimd.tensor_copy(k_part[:, 1, 0:width], k_rest[:, 0:width]))
                nc.gpsimd.tensor_tensor(k_part[:, 2, 0:width], k_rest[:, 0:width], k_part[:, 1, 0:width],
                                        ALU.subtract).then_inc(k_low, 1)
                pool.wait_ge(k_low, n + 1)

            def inverse_std(out_, var, eps_out, size):
                link(nc.gpsimd.tensor_scalar(eps_out, var, EPS, None, ALU.add))
                return nc.gpsimd.tensor_tensor(out_, eps_out, power[0:size, 0:out_.shape[1]], ALU.pow)

            for step in PLAN:
                if step[0] == "ln":
                    pool.wait_ge(var_ready, norms["hat", step[1]] + 1)
                    inverse_std(rstd[:, :], mean_var[:, :, 1], var_eps[:, :], P).then_inc(rstd_ready, 1)
                elif step[0] == "ctx_ln":
                    pool.wait_ge(var_ready, norms["ctx_hat"] + 1)
                    link(inverse_std(c_rstd[:, :, 0], c_mean_var[:, :, 0, 1], var_eps[:, 0:B], P))
                    inverse_std(c_rstd[0:TB, :, 1], c_mean_var[0:TB, :, 1, 1], var_eps[0:TB, 0:B], TB) \
                        .then_inc(rstd_ready, 1)
                elif step[0] == "k":
                    b = step[1]
                    k_split(b, S, (k_moved[0], 16 * len(K_PARTS)))
                    pool.wait_ge(tiles_cleared[b], 2)
                    for r, part in enumerate(K_PARTS):
                        pool.dma_start(k_tile[DH * r:DH * r + DH, b], k_part[:, part, :]).then_inc(k_moved[b], 16)
                elif step[0] == "ctx_k":
                    k_split(2, B * T, (k_moved[1], 16 * len(K_PARTS)))
                    pool.wait_ge(ctx_cleared, 1)
                    for b in range(B):
                        for r, part in enumerate(K_PARTS):
                            pool.dma_start(kc_tile[DH * r:DH * r + DH, b, :, 0:T],
                                           k_part[:, part, b * T:b * T + T]).then_inc(kc_moved, 16)
                elif step[0] == "mT":
                    g = step[1]
                    pool.wait_ge(neg_high, g + 1)
                    full, rest, part = neg_full[:, g % 2], neg_rest[:, g % 2], neg_part[:, g % 2]
                    link(nc.gpsimd.tensor_tensor(rest, full, part[:, 0], ALU.subtract))
                    link(nc.gpsimd.tensor_copy(part[:, 1], rest))
                    nc.gpsimd.tensor_tensor(part[:, 2], rest, part[:, 1], ALU.subtract).then_inc(neg_low, 1)

        @block.scalar
        def _(act):
            def col(c, n=P):
                return cols_sb[0:n, c:c + 1]

            def move_q(p):
                act.wait_ge(q_low, p + 1)
                act.wait_ge(tiles_cleared[p % 2], 2)
                for r, part in enumerate(Q_PARTS):
                    act.dma_start(q_tile[DH * r:DH * r + DH, p % 2], q_part[:, part, :]).then_inc(q_moved[p], 16)

            for step in PLAN:
                kind, n = step[0], step[-1]
                if kind in MISC_KINDS and kind not in ("oT", "proj", "router", "b2", "ctx_vB"):
                    act.wait_ge(misc_filled, MISC_USE[step] + 1)
                if kind == "hT":
                    g = (C_SA_G, C_CQ_G, C_MO_G)[n // 2]
                    act.wait_ge(cols_loaded, 16)
                    nc.scalar.activation(hT[:, n % 2], ps_x[:, :], ACT.Identity, bias=col(g + 1), scale=col(g)) \
                        .then_inc(misc_read, 1)
                elif kind == "q":
                    bias = col(C_SA_BQ if n < 2 else C_CA_BQ)
                    if n:
                        act.wait_ge(q_moved[n - 1], 16 * len(Q_PARTS))
                    nc.scalar.activation(q_part[:, 0], ps_x[:, :], ACT.Identity, bias=bias).then_inc(q_high, 1)
                    nc.scalar.activation(q_full[:, :], ps_x[:, :], ACT.Identity, bias=bias).then_inc(misc_read, 1)
                    move_q(n)
                elif kind in ("k", "ctx_k"):
                    m, width = (n, S) if kind == "k" else (2, B * T)
                    bias = col(C_SA_BK if kind == "k" else C_CA_BK)
                    if m:
                        act.wait_ge(k_moved[m - 1], 16 * len(K_PARTS))
                        act.wait_ge(k_low, m)
                    nc.scalar.activation(k_part[:, 0, 0:width], ps_x[:, 0:width], ACT.Identity, bias=bias)
                    nc.scalar.activation(k_full[:, 0:width], ps_x[:, 0:width], ACT.Identity, bias=bias) \
                        .then_inc(k_high, 1)
                    act.wait_ge(k_high, m + 1)
                    act.sem_inc(misc_read, 1)
                elif kind == "v":
                    nc.scalar.activation(v_aug[:, n, :, :, 0:DH],
                                         ps_x[:, :].rearrange("p (c h d) -> p c h d", c=QT, d=DH),
                                         ACT.Identity).then_inc(misc_read, 1)
                elif kind == "ctx_T":
                    nc.scalar.activation(ctxT[:, :], ps_x[:, 0:B * T], ACT.Identity, bias=col(C_KV_B),
                                         scale=col(C_KV_G)).then_inc(misc_read, 1)
                elif kind == "ctx_vA":
                    nc.scalar.activation(vc_aug[:, :, :, 0:DH],
                                         ps_x[:, 0:B * D].rearrange("p (b h d) -> p b h d", b=B, d=DH),
                                         ACT.Identity).then_inc(misc_read, 1)
                elif kind == "mT":
                    slot = n % 2
                    if n >= 2:
                        act.wait_ge(neg_moved[slot], 48 * (n // 2))
                    nc.scalar.activation(neg_part[:, slot, 0], ps_x[0:16, 0:P], ACT.Identity, scale=-1.0)
                    nc.scalar.activation(neg_full[:, slot], ps_x[0:16, 0:P], ACT.Identity, scale=-1.0) \
                        .then_inc(neg_high, 1)
                    act.wait_ge(neg_high, n + 1)
                    act.sem_inc(misc_read, 1)
                    act.wait_ge(neg_low, n + 1)
                    b, g = n // G % B, n % G
                    row = SELF_MAX_ROW if n < B * G else CROSS_MAX_ROW
                    for part in range(3):
                        act.dma_start(q_tile[row + part:row + part + 1, b, 4 * g:4 * g + 4, :],
                                      neg_part[:, slot, part]).then_inc(neg_moved[slot], 16)
                elif kind == "scores":
                    act.wait_ge(scored, n + 1)
                    if quad(n) >= 2:
                        act.wait_ge(pv_done, quad(n) - 1)
                    width = 512 if n >= SELF_UNITS and (n - SELF_UNITS) % 3 == 2 else 1024
                    lo = 2 * (n % 2)
                    nc.scalar.activation(probs[:, ring_slot(n), 0:width],
                                         ps_s[:, lo:lo + width // 512, :].rearrange("p a n -> p (a n)"),
                                         ACT.Exp, scale=SCALE).then_inc(exped, 1)
                elif kind == "pv" and (n >= 16 or n % 2):
                    g = n // 2 if n < 16 else n - 8
                    act.wait_ge(pv_done, n + 1)
                    if g >= 2:
                        act.wait_ge(misc_filled, MISC_USE[("oT", g - 2)] + 1)
                    nc.scalar.activation(o_raw[:, g % 2], ps_o[:, :], ACT.Identity).then_inc(o_copied, 1)
                elif kind == "osT":
                    nc.scalar.activation(oT[:, :], ps_x[:, :], ACT.Identity,
                                         bias=col(C_SA_BV if n < 2 else C_CA_BV)).then_inc(misc_read, 1)
                elif kind == "gates":
                    act.wait_ge(logits_shifted, n + 1)
                    nc.scalar.activation(expd[:, :, :], shifted[:, :, :], ACT.Exp).then_inc(logits_exped, 1)
                elif kind == "gT":
                    nc.scalar.activation(gateT[:, :], ps_x[0:E, :], ACT.Identity).then_inc(misc_read, 1)
                elif kind == "fc1":
                    for c in range(FC):
                        f = FC * n + c
                        act.wait_ge(fc1_done, f + 1)
                        if n >= 2 and c == 0:
                            act.wait_ge(fc2_done, n - 1)
                        h1 = probs[:, 2 * (n % 2) + c // 2, 512 * (c % 2):512 * (c % 2) + 512]
                        nc.scalar.activation(h1, ps_s[:, f % 4], ACT.Gelu,
                                             bias=col(C_FC1_B + FC * (n % E) + c)).then_inc(gelu_done, 1)

        @block.vector
        def _(dve):
            steps = [0]

            def link(ins):
                steps[0] += 1
                ins.then_inc(dve_chain, 1)
                dve.wait_ge(dve_chain, steps[0])

            nc.vector.memset(k_tile[:, 0].bitcast(F32), 0.0).then_inc(tiles_cleared[0], 1)

            for step in PLAN:
                kind, n = step[0], step[-1]
                if kind in ("oT", "proj", "router", "b2", "ctx_vB"):
                    dve.wait_ge(misc_filled, MISC_USE[step] + 1)
                if kind == "ln":
                    src = phase_input(n)
                    if n < 2:
                        dve.wait_ge(x_loaded[n], 16)
                    else:
                        dve.wait_ge(mid_ready, n - 1)
                        dve.wait_ge(misc_filled, MISC_USE[("hT", n - 1)] + 1)
                    if n == 1:
                        dve.wait_ge(misc_filled, MISC_USE[("hT", 0)] + 1)
                    for t in range(QT):
                        ins = nc.vector.bn_stats(stats[:, t], src[:, t])
                    link(ins)
                    for t in range(QT):
                        ins = nc.vector.bn_aggr(mean_var[:, t], stats[:, t])
                    ins.then_inc(var_ready, 1)
                elif kind == "hat":
                    src = phase_input(n)
                    dve.wait_ge(rstd_ready, norms["hat", n] + 1)
                    for t in range(QT):
                        ins = nc.vector.tensor_scalar(x_hat[:, t], src[:, t], mean_var[:, t, 0:1], rstd[:, t:t + 1],
                                                      ALU.subtract, ALU.mult)
                    ins.then_inc(hat_ready, 1)
                elif kind == "ctx_ln":
                    dve.wait_ge(ctx_loaded, 32)
                    for c, size in ((0, P), (1, TB)):
                        for b in range(B):
                            ins = nc.vector.bn_stats(c_stats[0:size, b, c], ctx_sb[0:size, b, c])
                    link(ins)
                    for c, size in ((0, P), (1, TB)):
                        for b in range(B):
                            ins = nc.vector.bn_aggr(c_mean_var[0:size, b, c], c_stats[0:size, b, c])
                    ins.then_inc(var_ready, 1)
                elif kind == "ctx_hat":
                    dve.wait_ge(rstd_ready, norms["ctx_hat"] + 1)
                    for c, size in ((0, P), (1, TB)):
                        for b in range(B):
                            ins = nc.vector.tensor_scalar(c_hat[0:size, b, c], ctx_sb[0:size, b, c],
                                                          c_mean_var[0:size, b, c, 0:1], c_rstd[0:size, b, c:c + 1],
                                                          ALU.subtract, ALU.mult)
                    ins.then_inc(ctx_hat_ready, 1)
                elif kind == "q":
                    dve.wait_ge(misc_read, MISC_USE[step] + 1)
                    link(nc.vector.tensor_tensor(q_rest[:, :], q_full[:, :], q_part[:, 0], ALU.subtract))
                    link(nc.vector.tensor_copy(q_part[:, 1], q_rest[:, :]))
                    nc.vector.tensor_tensor(q_part[:, 2], q_rest[:, :], q_part[:, 1], ALU.subtract).then_inc(q_low, 1)
                elif kind == "ctx_vB":
                    dve.wait_ge(ctx_cleared, 7)
                    for b in range(B):
                        for j in range(4):
                            rows_j = slice(32 * j, 32 * j + TB)
                            src = ps_x[rows_j, b * D:b * D + D].rearrange("p (g j d) -> p g j d", g=G, j=4)[:, :, j]
                            ins = nc.vector.tensor_copy(vc_diag[rows_j, b, :, j, 0:DH], src)
                    ins.then_inc(misc_read, 1)
                elif kind == "max":
                    dve.wait_ge(max_filled, n + 1)
                    if n < SELF_MAX:
                        nc.vector.tensor_reduce(row_max[:, n // 16, n % 16:n % 16 + 1], ps_m[:, n % 2], AX.X,
                                                ALU.max).then_inc(max_read, 1)
                    else:
                        c, i = (n - SELF_MAX) // 8, (n - SELF_MAX) % 8
                        t, pair = i // 2, i % 2
                        dst = row_max[:, 8 + c].rearrange("p (h t) -> p h t", t=QT)[:, 2 * pair:2 * pair + 2, t]
                        nc.vector.tensor_reduce(dst, ps_m[:, n % 2, 0:2 * T].rearrange("p (h k) -> p h k", k=T),
                                                AX.X, ALU.max).then_inc(max_read, 1)
                elif kind == "oT":
                    raw = ps_x[:, :].rearrange("p (t j c) -> p t j c", t=QT, j=4)
                    b, g = n // G % B, n % G
                    link(nc.vector.reciprocal(o_rden[:, :, :], raw[:, :, :, DH]))
                    ins = nc.vector.tensor_tensor(o_tok[:, b, :, 4 * g:4 * g + 4, :], raw[:, :, :, 0:DH],
                                                  o_rden[:, :, :].unsqueeze(3).to_broadcast([P, QT, 4, DH]), ALU.mult)
                    ins.then_inc(misc_read, 1)
                    dve.wait_ge(misc_read, MISC_USE[step] + 1)
                    if g == G - 1:
                        dve.sem_inc(o_normed, 1)
                elif kind == "proj":
                    b = n % B
                    src, dst = (x_sb, x_mid) if n < 2 else (x_mid, x_out)
                    row = R_SA_OUT if n < 2 else R_CA_OUT
                    dve.wait_ge(rows_loaded, 16)
                    link(nc.vector.tensor_tensor(dst[:, b], src[:, b],
                                                 rows_sb[:, row:row + D].unsqueeze(1).to_broadcast([P, QT, D]), ALU.add))
                    nc.vector.tensor_tensor(dst[:, b], ps_x[:, :].rearrange("p (t d) -> p t d", t=QT), dst[:, b],
                                            ALU.add).then_inc(misc_read, 1)
                    dve.wait_ge(misc_read, MISC_USE[step] + 1)
                    dve.sem_inc(mid_ready, 1)
                elif kind == "router":
                    link(nc.vector.tensor_tensor(logit[:, :, :], ps_x[:, 0:QT * E].rearrange("p (t e) -> p t e", t=QT),
                                                 rows_sb[:, R_ROUTER:R_ROUTER + E].unsqueeze(1)
                                                 .to_broadcast([P, QT, E]), ALU.add))
                    dve.sem_inc(misc_read, 1)
                    link(nc.vector.tensor_reduce(top[:, :], logit[:, :, :], AX.X, ALU.max))
                    nc.vector.tensor_tensor(shifted[:, :, :], logit[:, :, :],
                                            top[:, :].unsqueeze(2).to_broadcast([P, QT, E]),
                                            ALU.subtract).then_inc(logits_shifted, 1)
                elif kind == "gates":
                    dve.wait_ge(lower_ready, 1)
                    for t in range(QT):
                        own = logit[:, t].unsqueeze(2).to_broadcast([P, E, E])
                        other = logit[:, t].unsqueeze(1).to_broadcast([P, E, E])
                        nc.vector.tensor_tensor(beats[:, :, :], other, own, ALU.is_gt)
                        link(nc.vector.tensor_tensor(ties[:, :, :], other, own, ALU.is_equal))
                        link(nc.vector.tensor_tensor(ties[:, :, :], ties[:, :, :], lower[:, :, :], ALU.mult))
                        link(nc.vector.tensor_tensor(beats[:, :, :], beats[:, :, :], ties[:, :, :], ALU.add))
                        link(nc.vector.tensor_reduce(rank[:, t], beats[:, :, :], AX.X, ALU.add))
                    dve.wait_ge(logits_exped, n + 1)
                    link(nc.vector.scalar_tensor_tensor(out=kept[:, :, :], in0=rank[:, :, :], scalar=2.0,
                                                        in1=expd[:, :, :], op0=ALU.is_lt, op1=ALU.mult))
                    link(nc.vector.tensor_reduce(gsum[:, :], kept[:, :, :], AX.X, ALU.add))
                    link(nc.vector.reciprocal(grec[:, :], gsum[:, :]))
                    nc.vector.tensor_tensor(gate[:, n], kept[:, :, :], grec[:, :].unsqueeze(2)
                                            .to_broadcast([P, QT, E]), ALU.mult).then_inc(gates_ready, 1)
                elif kind == "b2":
                    nc.vector.tensor_tensor(x_out[:, n], ps_x[:, :].rearrange("p (t d) -> p t d", t=QT), x_out[:, n],
                                            ALU.add).then_inc(misc_read, 1)
                elif kind == "fc2":
                    b, e = n // E, n % E
                    dve.wait_ge(fc2_done, n + 1)
                    if e:
                        dve.wait_ge(combined, n)
                    else:
                        dve.wait_ge(misc_read, MISC_USE[("b2", b)] + 1)
                    for t in range(QT):
                        ins = nc.vector.scalar_tensor_tensor(out=x_out[:, b, t], in0=ps_m[:, n % 2, t * D:t * D + D],
                                                             scalar=gate[:, b, t, e:e + 1], in1=x_out[:, b, t],
                                                             op0=ALU.mult, op1=ALU.add)
                    ins.then_inc(combined, 1)

        @block.tensor
        def _(pe):
            pe.wait_ge(ident_ready, 1)

            def transposes(src, cols_of, rows_in=P):
                for t in range(QT):
                    mm = nc.tensor.transpose(ps_x[0:cols_of, t * P:t * P + rows_in], src(t), ident[0:rows_in, 0:rows_in])
                return mm

            for step in PLAN:
                kind, n = step[0], step[-1]
                if kind in MISC_KINDS and MISC_USE[step]:
                    pe.wait_ge(misc_read, MISC_USE[step])
                mm = None
                if kind == "hT":
                    pe.wait_ge(hat_ready, n + 1)
                    mm = transposes(lambda t: x_hat[:, t], P)
                elif kind == "q":
                    a = 0 if n < 2 else 1
                    pe.wait_ge(w_in_loaded, 16)
                    pe.wait_ge(misc_read, MISC_USE[("hT", n)] + 1)
                    mm = nc.tensor.matmul(ps_x[:, :], w_in_sb[:, a, 0:D], hT[:, n % 2], start=True, stop=True)
                elif kind == "k":
                    mm = nc.tensor.matmul(ps_x[:, :], w_in_sb[:, 0, D:2 * D], hT[:, n], start=True, stop=True)
                elif kind == "v":
                    for c in range(QT):
                        mm = nc.tensor.matmul(ps_x[:, c * D:c * D + D], hT[:, n, c * P:c * P + P],
                                              w_in_sb[:, 0, 2 * D:3 * D], start=True, stop=True)
                elif kind == "ctx_T":
                    pe.wait_ge(ctx_hat_ready, 1)
                    for b in range(B):
                        nc.tensor.transpose(ps_x[:, b * T:b * T + P], c_hat[:, b, 0], ident[:, :])
                        mm = nc.tensor.transpose(ps_x[:, b * T + P:b * T + T], c_hat[0:TB, b, 1], ident[0:TB, 0:TB])
                elif kind == "ctx_k":
                    mm = nc.tensor.matmul(ps_x[:, 0:B * T], w_in_sb[:, 1, D:2 * D], ctxT[:, :], start=True, stop=True)
                elif kind == "ctx_vA":
                    for b in range(B):
                        mm = nc.tensor.matmul(ps_x[:, b * D:b * D + D], ctxT[:, b * T:b * T + P],
                                              w_in_sb[:, 1, 2 * D:3 * D], start=True, stop=True)
                elif kind == "ctx_vB":
                    for b in range(B):
                        for j in range(4):
                            mm = nc.tensor.matmul(ps_x[32 * j:32 * j + TB, b * D:b * D + D],
                                                  ctxT[:, b * T + P:b * T + T], w_in_sb[:, 1, 2 * D:3 * D],
                                                  start=True, stop=True, tile_position=(0, 32 * j))
                elif kind == "max":
                    if n >= 2:
                        pe.wait_ge(max_read, n - 1)
                    if n < SELF_MAX:
                        b, h, t = n // 64, n % 64 // 4, n % 4
                        if n % 64 == 0:
                            pe.wait_ge(q_moved[b], 16 * len(Q_PARTS))
                            pe.wait_ge(k_moved[b], 16 * len(K_PARTS))
                            pe.wait_ge(key_ones[b], 16 * 4)
                        mm = nc.tensor.matmul(ps_m[:, n % 2], q_tile[:, b, h, t * P:t * P + P], k_tile[:, b, h],
                                              start=True, stop=True)
                    else:
                        c, i = (n - SELF_MAX) // 8, (n - SELF_MAX) % 8
                        b, t, pair = c // G, i // 2, i % 2
                        if c % G == 0 and i == 0:
                            pe.wait_ge(q_moved[2 + b], 16 * len(Q_PARTS))
                            pe.wait_ge(kc_moved, 16 * B * len(K_PARTS))
                            pe.wait_ge(ctx_key_ones, 16 * 4)
                        for k in range(2):
                            h = 4 * (c % G) + 2 * pair + k
                            mm = nc.tensor.matmul(ps_m[:, n % 2, k * T:k * T + T], q_tile[:, b, h, t * P:t * P + P],
                                                  kc_tile[:, b, h, 0:T], start=True, stop=True)
                    mm.then_inc(max_filled, 1)
                    mm = None
                elif kind == "mT":
                    pe.wait_ge(max_read, max_until(n))
                    mm = nc.tensor.transpose(ps_x[0:16, 0:P], row_max[:, n], ident[:, :])
                elif kind == "scores":
                    g = group_of(n)
                    pe.wait_ge(neg_moved[g % 2], 48 * (g // 2 + 1))
                    if n >= 2:
                        pe.wait_ge(exped, n - 1)
                    lo = 2 * (n % 2)
                    if n < SELF_UNITS:
                        b, g, half, j = n // 32, n // 8 % G, n % 8 // 4, n % 4
                        h = 4 * g + j
                        for k in range(2):
                            c = 2 * half + k
                            mm = nc.tensor.matmul(ps_s[:, lo + k], k_tile[:, b, h, c * P:c * P + P], q_tile[:, b, h],
                                                  start=True, stop=True)
                    else:
                        c, i = (n - SELF_UNITS) // 3, (n - SELF_UNITS) % 3
                        b = c // G
                        for k in range(2 if i < 2 else 4):
                            h = 4 * (c % G) + (2 * i + k if i < 2 else k)
                            if i < 2:
                                mm = nc.tensor.matmul(ps_s[:, lo + k], kc_tile[:, b, h, 0:P], q_tile[:, b, h],
                                                      start=True, stop=True)
                            else:
                                mm = nc.tensor.matmul(ps_s[32 * k:32 * k + 32, lo], kc_tile[:, b, h, P:TP],
                                                      q_tile[:, b, h], start=True, stop=True,
                                                      tile_position=(0, 32 * k))
                    mm.then_inc(scored, 1)
                    mm = None
                elif kind == "pv":
                    pe.wait_ge(exped, units_until(n))
                    if n < 16:
                        b, g, half = n // 8, n // 2 % G, n % 2
                        if half == 0 and n:
                            pe.wait_ge(o_copied, n // 2)
                        if n % 8 == 0:
                            pe.wait_ge(misc_read, MISC_USE[("v", b)] + 1)
                            pe.wait_ge(v_cleared, 2 * (b + 1))
                        for k in range(2):
                            for j in range(4):
                                mm = nc.tensor.matmul(ps_o[32 * j:32 * j + 32, :], v_aug[:, b, 2 * half + k, 4 * g + j],
                                                      probs[:, (4 * n + j) % 8, 512 * k:512 * k + 512],
                                                      start=(half == 0 and k == 0), stop=(half == 1 and k == 1),
                                                      tile_position=(0, 32 * j), skip_group_check=True)
                    else:
                        c = n - 16
                        b, g = c // G, c % G
                        pe.wait_ge(o_copied, n - 8)
                        if c == 0:
                            pe.wait_ge(misc_read, MISC_USE[("ctx_vB",)] + 1)
                            pe.wait_ge(ctx_cleared, 7)
                        nc.tensor.matmul(ps_o[:, :], vc_diag[:, b, g].rearrange("p j c -> p (j c)"),
                                         probs[:, ring_slot(SELF_UNITS + 3 * c + 2), 0:512],
                                         start=True, stop=False, skip_group_check=True)
                        for j in range(4):
                            mm = nc.tensor.matmul(ps_o[32 * j:32 * j + 32, :], vc_aug[:, b, 4 * g + j],
                                                  probs[:, ring_slot(SELF_UNITS + 3 * c + j // 2),
                                                        512 * (j % 2):512 * (j % 2) + 512],
                                                  start=False, stop=True, tile_position=(0, 32 * j),
                                                  skip_group_check=True)
                    mm.then_inc(pv_done, 1)
                    mm = None
                elif kind == "oT":
                    pe.wait_ge(o_copied, n + 1)
                    mm = transposes(lambda t: o_raw[:, n % 2, t * P:t * P + P], P)
                elif kind == "osT":
                    pe.wait_ge(o_normed, n + 1)
                    mm = transposes(lambda t: o_tok[:, n % 2, t].rearrange("p h d -> p (h d)"), P)
                elif kind == "proj":
                    pe.wait_ge(w_out_loaded, 16)
                    pe.wait_ge(misc_read, MISC_USE[("osT", n)] + 1)
                    for t in range(QT):
                        mm = nc.tensor.matmul(ps_x[:, t * D:t * D + D], oT[:, t * P:t * P + P], w_out_sb[:, n // 2],
                                              start=True, stop=True)
                elif kind == "router":
                    pe.wait_ge(misc_read, MISC_USE[("hT", 4 + n)] + 1)
                    for t in range(QT):
                        mm = nc.tensor.matmul(ps_x[:, t * E:t * E + E], hT[:, n, t * P:t * P + P],
                                              cols_sb[:, C_ROUTER:C_ROUTER + E], start=True, stop=True)
                elif kind == "gT":
                    pe.wait_ge(gates_ready, n + 1)
                    mm = transposes(lambda t: gate[:, n, t], E)
                elif kind == "b2":
                    pe.wait_ge(fc2_b_loaded, 16)
                    pe.wait_ge(misc_read, MISC_USE[("gT", n)] + 1)
                    for t in range(QT):
                        mm = nc.tensor.matmul(ps_x[:, t * D:t * D + D], gateT[:, t * P:t * P + P], fc2_b_sb[:, :],
                                              start=True, stop=True)
                elif kind == "fc1":
                    b, e = n // E, n % E
                    if n == 0:
                        pe.wait_ge(fc1_loaded, 16)
                        pe.wait_ge(exped, UNITS)
                    if e == 0:
                        pe.wait_ge(misc_read, MISC_USE[("hT", 4 + b)] + 1)
                    for c in range(FC):
                        f = FC * n + c
                        if f >= 4:
                            pe.wait_ge(gelu_done, f - 3)
                        nc.tensor.matmul(ps_s[:, f % 4], fc1_sb[:, e, c * P:c * P + P], hT[:, b],
                                         start=True, stop=True).then_inc(fc1_done, 1)
                elif kind == "fc2":
                    b, e = n // E, n % E
                    if n == 0:
                        pe.wait_ge(fc2_loaded, 16)
                        pe.wait_ge(max_read, SELF_MAX + CROSS_MAX)
                    pe.wait_ge(gelu_done, FC * (n + 1))
                    if n >= 2:
                        pe.wait_ge(combined, n - 1)
                    for t in range(QT):
                        for c in range(FC):
                            lo = 512 * (c % 2) + t * P
                            mm = nc.tensor.matmul(ps_m[:, n % 2, t * D:t * D + D],
                                                  probs[:, 2 * (n % 2) + c // 2, lo:lo + P], fc2_sb[:, e, c],
                                                  start=(c == 0), stop=(c == FC - 1))
                    mm.then_inc(fc2_done, 1)
                    mm = None
                if mm is not None:
                    mm.then_inc(misc_filled, 1)


def kernel(x, ctx_1024, L0_xattn_sa_ln_g, L0_xattn_sa_ln_b, L0_xattn_sa_in_w, L0_xattn_sa_in_b, L0_xattn_sa_out_w,
           L0_xattn_sa_out_b, L0_xattn_ca_q_ln_g, L0_xattn_ca_q_ln_b, L0_xattn_ca_kv_ln_g, L0_xattn_ca_kv_ln_b,
           L0_xattn_ca_in_w, L0_xattn_ca_in_b, L0_xattn_ca_out_w, L0_xattn_ca_out_b, L0_xattn_moe_ln_g,
           L0_xattn_moe_ln_b, L0_xattn_router_w, L0_xattn_router_b, L0_xattn_e_fc1_w, L0_xattn_e_fc1_b,
           L0_xattn_e_fc2_w, L0_xattn_e_fc2_b):
    import numpy as np
    import concourse.bacc as bacc
    from concourse import mybir as mb
    from concourse.bass_utils import run_bass_kernel_spmd

    def head_minor(a):
        return np.asarray(a).reshape(H, DH, -1).transpose(1, 0, 2).reshape(D, -1)

    def w_in(a):
        a = np.asarray(a)
        return np.concatenate([head_minor(a[0:D]), head_minor(a[D:2 * D]), a[2 * D:]], axis=0).T

    def b_in(a):
        a = np.asarray(a)
        return [head_minor(a[0:D])[:, 0], head_minor(a[D:2 * D])[:, 0], a[2 * D:]]

    cols = np.stack([np.asarray(a) for a in (
        L0_xattn_sa_ln_g, L0_xattn_sa_ln_b, L0_xattn_ca_q_ln_g, L0_xattn_ca_q_ln_b, L0_xattn_ca_kv_ln_g,
        L0_xattn_ca_kv_ln_b, L0_xattn_moe_ln_g, L0_xattn_moe_ln_b, *b_in(L0_xattn_sa_in_b), *b_in(L0_xattn_ca_in_b))]
        + [a for a in np.asarray(L0_xattn_e_fc1_b).reshape(E * FC, P)]
        + [a for a in np.asarray(L0_xattn_router_w)], axis=1)
    rows = np.concatenate([np.asarray(L0_xattn_sa_out_b), np.asarray(L0_xattn_ca_out_b),
                           np.asarray(L0_xattn_router_b)])
    arrays = {
        "x": np.asarray(x),
        "ctx_in": np.asarray(ctx_1024),
        "w_in": np.stack([w_in(L0_xattn_sa_in_w), w_in(L0_xattn_ca_in_w)], axis=1),
        "w_out": np.stack([np.asarray(L0_xattn_sa_out_w).T, np.asarray(L0_xattn_ca_out_w).T], axis=1),
        "cols": cols,
        "rows": rows,
        "fc1_w": np.asarray(L0_xattn_e_fc1_w).transpose(2, 0, 1),
        "fc2_w": np.asarray(L0_xattn_e_fc2_w).reshape(E, D, FC, P).transpose(3, 0, 2, 1),
        "fc2_b": np.asarray(L0_xattn_e_fc2_b),
    }
    arrays = {k: np.ascontiguousarray(a) for k, a in arrays.items()}
    nc = bacc.Bacc("TRN2", target_bir_lowering=False, num_devices=1)
    args = [nc.dram_tensor(k, a.shape, mb.dt.from_np(a.dtype), kind="ExternalInput").ap() for k, a in arrays.items()]
    out = nc.dram_tensor("out", (B, S, D), F32, kind="ExternalOutput").ap()
    build(nc, *args, out)
    result = run_bass_kernel_spmd(nc, [arrays], core_ids=[0])
    return result.results[0]["out"]
```

```python
from contextlib import ExitStack

import concourse.bass as bass
from concourse import mybir

F32 = mybir.dt.float32
BF16 = mybir.dt.bfloat16
ALU = mybir.AluOpType
ACT = mybir.ActivationFunctionType
AX = mybir.AxisListType

P = 128
B, S, D = 2, 512, 128
T = 154
H, DH = 16, 8
E, FF = 8, 512
EPS = 1e-5
QT = S // P
FC = FF // P
TB = T - P
TP = 160
G = H // 4
SCALE = float(DH) ** -0.5

Q_PARTS = (0, 0, 1, 1, 0, 2)
K_PARTS = (0, 1, 0, 1, 2, 0)
SELF_MAX_ROW = DH * len(Q_PARTS)
CROSS_MAX_ROW = SELF_MAX_ROW + 3

(C_SA_G, C_SA_B, C_CQ_G, C_CQ_B, C_KV_G, C_KV_B, C_MO_G, C_MO_B,
 C_SA_BQ, C_SA_BK, C_SA_BV, C_CA_BQ, C_CA_BK, C_CA_BV) = range(14)
C_FC1_B = 14
C_ROUTER = C_FC1_B + E * FC
N_COLS = C_ROUTER + E
R_SA_OUT, R_CA_OUT, R_ROUTER = 0, D, 2 * D
N_ROWS = 2 * D + E

SELF_UNITS = B * H * 2
LEAD = 12
SELF_MAX = B * H * QT
CROSS_MAX = B * G * 8


def make_plan():
    plan = []
    add = plan.append

    def maxima(lo, n):
        for i in range(lo, lo + n):
            add(("max", i))

    plan.extend([("ln", 0), ("hat", 0), ("hT", 0), ("k", 0), ("q", 0), ("v", 0)])
    maxima(0, 16)
    add(("neg", 0))
    maxima(16, 1)
    add(("mT", 0))
    maxima(17, 2 * LEAD - 17)

    beside = {0: [("ln", 1)], 2: [("hat", 1)], 4: [("hT", 1)], 5: [("ctx_ln",)], 6: [("q", 1)], 8: [("k", 1)],
              9: [("ctx_hat",)], 10: [("v", 1)], 12: [("ctx_T",)], 15: [("ctx_k",)], 17: [("ctx_vA",)],
              19: [("ctx_vB",)], 33: [("load_fc1",)],
              40: [("osT", 0)], 42: [("proj", 0)], 43: [("ln", 2)], 44: [("hat", 2)], 46: [("hT", 2)],
              48: [("q", 2)], 57: [("neg", 8)], 58: [("mT", 8)], 61: [("neg", 9)], 62: [("mT", 9)],
              63: [("load_fc2",)]}
    for u in range(SELF_UNITS):
        n = 2 * (u + LEAD)
        if n < SELF_MAX:
            maxima(n, 2)
        elif u >= 54:
            maxima(SELF_MAX + 2 * (u - 54), 2 if u < 62 else 0)
        add(("scores", u))
        if u % 8 == 3 and u + 5 < SELF_UNITS:
            add(("neg", (u + 5) // 8))
        if u % 8 == 5 and u + 3 < SELF_UNITS:
            add(("mT", (u + 3) // 8))
        if u % 4 == 3 and u >= 7:
            add(("pv", u // 4 - 1))
        if u % 8 == 6 and u >= 14:
            add(("oT", u // 8 - 1))
        plan.extend(beside.get(u, []))

    def cross(v):
        add(("scores", SELF_UNITS + v))

    add(("pv", 15))
    maxima(SELF_MAX + 16, 4)
    cross(0)
    add(("oT", 7))
    maxima(SELF_MAX + 20, 4)
    cross(1)
    add(("neg", 10))
    add(("osT", 1))
    cross(2)
    add(("mT", 10))
    add(("proj", 1))
    add(("ln", 3))
    maxima(SELF_MAX + 24, 4)
    cross(3)
    add(("hat", 3))
    add(("pv", 16))
    maxima(SELF_MAX + 28, 4)
    add(("hT", 3))
    add(("neg", 11))
    cross(4)
    add(("q", 3))
    cross(5)
    add(("oT", 8))
    add(("mT", 11))
    add(("pv", 17))
    cross(6)
    cross(7)
    cross(8)
    add(("oT", 9))
    add(("pv", 18))
    cross(9)
    cross(10)
    cross(11)
    add(("pv", 19))
    add(("oT", 10))
    maxima(SELF_MAX + 32, 4)
    add(("oT", 11))
    maxima(SELF_MAX + 36, 4)
    add(("neg", 12))
    add(("osT", 2))
    maxima(SELF_MAX + 40, 2)
    add(("mT", 12))
    maxima(SELF_MAX + 42, 6)
    add(("proj", 2))
    add(("ln", 4))
    add(("neg", 13))
    add(("mT", 13))
    add(("hat", 4))
    maxima(SELF_MAX + 48, 4)
    cross(12)
    cross(13)
    cross(14)
    add(("hT", 4))
    maxima(SELF_MAX + 52, 4)
    add(("neg", 14))
    cross(15)
    add(("pv", 20))
    add(("router", 0))
    add(("mT", 14))
    cross(16)
    cross(17)
    add(("oT", 12))
    add(("gates", 0))

    last = SELF_UNITS + 3 * 6
    after_fc1 = {0: [("gT", 0), ("pv", 21)], 1: [("b2", 0), ("oT", 13)], 2: [("mT", 15), ("pv", 22)],
                 3: [("scores", last + 3), ("scores", last + 4), ("scores", last + 5), ("oT", 14)],
                 4: [("pv", 23)], 5: [("oT", 15)], 6: [("proj", 3), ("ln", 5)], 7: [("hT", 5)],
                 8: [("gates", 1)], 9: [("b2", 1)]}
    after_fc2 = {0: [("scores", last)], 1: [("scores", last + 1), ("scores", last + 2), ("neg", 15)],
                 5: [("osT", 3)], 6: [("hat", 5)], 7: [("router", 1)], 8: [("gT", 1)]}
    for n in range(B * E):
        add(("fc1", n))
        plan.extend(after_fc1.get(n, []))
        if n < 2:
            maxima(SELF_MAX + 56 + 4 * n, 4)
        if n:
            add(("fc2", n - 1))
        if n == E:
            add(("store", 0))
        plan.extend(after_fc2.get(n, []))
    add(("fc2", B * E - 1))
    add(("store", 1))
    return plan


PLAN = make_plan()
MISC_KINDS = ("hT", "q", "k", "v", "ctx_T", "ctx_k", "ctx_vA", "ctx_vB", "mT", "oT", "osT", "proj", "router", "gT", "b2")
MISC_USE = {step: n for n, step in enumerate(s for s in PLAN if s[0] in MISC_KINDS and s != ("k", 0))}
def pieces_of(u):
    if u < SELF_UNITS:
        return range(2 * u, 2 * u + 2)
    c, i = (u - SELF_UNITS) // 3, (u - SELF_UNITS) % 3
    first = 2 * SELF_UNITS + 5 * c + 2 * i
    return range(first, first + (2 if i < 2 else 1))


def probs_slot(m):
    if m < 2 * SELF_UNITS:
        return m % 16
    return (8 * ((m - 2 * SELF_UNITS) // 5) + (m - 2 * SELF_UNITS) % 5) % 16


def quad(m):
    return m // 8 if m < 2 * SELF_UNITS else SELF_UNITS // 4 + (m - 2 * SELF_UNITS) // 5


def last_piece(q):
    return 8 * q + 7 if q < SELF_UNITS // 4 else 2 * SELF_UNITS + 5 * (q - SELF_UNITS // 4) + 4


def last_max(g):
    return 16 * g + 15 if g < 8 else SELF_MAX + 8 * (g - 8) + 7


def number_banks():
    s_ring, m_ring = {}, {}
    for kind, n in (step for step in PLAN if len(step) == 2):
        if kind == "scores":
            for m in pieces_of(n):
                s_ring["scores", m] = len(s_ring)
        elif kind == "fc1":
            for c in range(FC):
                s_ring["fc1", FC * n + c] = len(s_ring)
        elif kind in ("max", "fc2"):
            m_ring[kind, n] = len(m_ring)
    return s_ring, m_ring


S_RING, M_RING = number_banks()


def group_of(w):
    return w // 8 if w < SELF_UNITS else 8 + (w - SELF_UNITS) // 3


def build(nc, x, ctx_in, w_in, w_out, cols, rows, fc1_w, fc2_w, fc2_b, out):
    ctx = ExitStack()
    with ctx:
        def sb(name, shape, dt=F32):
            return ctx.enter_context(nc.sbuf_tensor(name, shape, dt))

        def sem(name):
            return ctx.enter_context(nc.semaphore(name))

        x_sb = sb("x_sb", [P, B, QT, D])
        ctx_sb = sb("ctx_sb", [P, B, 2, D])
        w_in_sb = sb("w_in_sb", [P, 2, 3 * D])
        w_out_sb = sb("w_out_sb", [P, 2, D])
        cols_sb = sb("cols_sb", [P, N_COLS])
        rows_sb = sb("rows_sb", [P, N_ROWS])
        fc2_b_sb = sb("fc2_b_sb", [E, D])
        ident = sb("ident", [P, P])
        ones_row = sb("ones_row", [3, H * S // 4], BF16)
        power = sb("power", [P, QT])
        zero = sb("zero", [P, 1])
        lower = sb("lower", [P, E, E])
        q_tile = sb("q_tile", [P, B, H, S], BF16)
        k_tile = sb("k_tile", [P, B, H, S], BF16)
        fc1_sb = k_tile[:, 0].bitcast(F32).rearrange("p (e a) n -> p e (a n)", e=E)
        fc2_sb = k_tile[:, 1].bitcast(F32).rearrange("p (e a) n -> p e (a n)", e=E) \
            .rearrange("p e (c d) -> p e c d", c=FC)
        kc_tile = sb("kc_tile", [P, B, H, TP], BF16)
        v_aug = sb("v_aug", [P, B, QT, H, 32])
        hidden = v_aug[:, :, :, :, :].rearrange("p b c h w -> p (b c) (h w)")
        vc_aug = sb("vc_aug", [P, B, H, 32])
        vc_diag = sb("vc_diag", [P, B, G, 4, 32])
        probs = sb("probs", [P, 16, 512])
        q_rest = sb("q_rest", [P, S])
        q_part = sb("q_part", [P, 3, S], BF16)
        k_full, k_rest = sb("k_full", [P, S]), sb("k_rest", [P, S])
        k_part = sb("k_part", [P, 3, S], BF16)
        row_max = sb("row_max", [P, 16, 16])
        neg_full, neg_rest = sb("neg_full", [P, 16]), sb("neg_rest", [P, 16])
        neg_part = sb("neg_part", [P, 3, 16], BF16)
        neg_rows = sb("neg_rows", [48, 2, P], BF16)
        ident_bf = sb("ident_bf", [P, P], BF16)
        stats = sb("stats", [P, QT, 6])
        mean_var = sb("mean_var", [P, QT, 2])
        rstd = sb("rstd", [P, QT])
        x_hat = sb("x_hat", [P, QT, D])
        c_stats = sb("c_stats", [P, B, 2, 6])
        c_mean_var = sb("c_mean_var", [P, B, 2, 2])
        c_rstd = sb("c_rstd", [P, B, 2])
        var_eps = sb("var_eps", [P, QT])
        c_hat = sb("c_hat", [P, B, 2, D])
        hT = sb("hT", [P, 2, S])
        ctxT = sb("ctxT", [P, B * T])
        o_raw = sb("o_raw", [P, 2, S])
        o_rden = sb("o_rden", [P, QT, 4])
        o_tok = sb("o_tok", [P, 2, QT, H, DH])
        oT = sb("oT", [P, S])
        x_mid = sb("x_mid", [P, B, QT, D])
        x_out = sb("x_out", [P, B, QT, D])
        logit = sb("logit", [P, QT, E])
        beats = sb("beats", [P, E, E])
        ties = sb("ties", [P, E, E])
        rank = sb("rank", [P, QT, E])
        top = sb("top", [P, QT])
        shifted = sb("shifted", [P, QT, E])
        expd = sb("expd", [P, QT, E])
        kept = sb("kept", [P, QT, E])
        gsum = sb("gsum", [P, QT])
        grec = sb("grec", [P, QT])
        gate = sb("gate", [P, B, QT, E])
        gateT = sb("gateT", [E, S])

        ps_s = ctx.enter_context(nc.psum_tensor("ps_s", [P, 3, 512], F32))
        ps_m = ctx.enter_context(nc.psum_tensor("ps_m", [P, 3, 512], F32))
        ps_o = ctx.enter_context(nc.psum_tensor("ps_o", [P, 512], F32))
        ps_x = ctx.enter_context(nc.psum_tensor("ps_x", [P, 512], F32))

        x_loaded = [sem(f"x_loaded{b}") for b in range(B)]
        ctx_loaded, w_in_loaded, w_out_loaded = sem("ctx_loaded"), sem("w_in_loaded"), sem("w_out_loaded")
        cols_loaded, rows_loaded = sem("cols_loaded"), sem("rows_loaded")
        fc1_loaded, fc2_loaded, fc2_b_loaded = sem("fc1_loaded"), sem("fc2_loaded"), sem("fc2_b_loaded")
        zero_ready = sem("zero_ready")
        ident_ready, ones_ready, lower_ready = sem("ident_ready"), sem("ones_ready"), sem("lower_ready")
        tiles_cleared = [sem(f"tiles_cleared{b}") for b in range(B)]
        ctx_cleared, v_cleared = sem("ctx_cleared"), sem("v_cleared")
        k0_filled = sem("k0_filled")
        key_ones = [sem(f"key_ones{b}") for b in range(B)]
        ctx_key_ones = sem("ctx_key_ones")
        pool_chain = sem("pool_chain")
        dve_chain = sem("dve_chain")
        misc_filled = sem("misc_filled")
        misc_read = sem("misc_read")
        var_ready = sem("var_ready")
        rstd_ready = sem("rstd_ready")
        hat_ready = sem("hat_ready")
        ctx_hat_ready = sem("ctx_hat_ready")
        hT_ready, ctxT_ready = sem("hT_ready"), sem("ctxT_ready")
        q_high = sem("q_high")
        q_low = sem("q_low")
        k_high, k_low = sem("k_high"), sem("k_low")
        q_moved = [sem(f"q_moved{p}") for p in range(4)]
        k_moved = [sem(f"k_moved{b}") for b in range(B)]
        kc_moved = sem("kc_moved")
        v_ready, vc_ready, vd_ready = sem("v_ready"), sem("vc_ready"), sem("vd_ready")
        m_filled, m_read = sem("m_filled"), sem("m_read")
        neg_split, neg_turned = sem("neg_split"), sem("neg_turned")
        neg_moved = [sem(f"neg_moved{i}") for i in range(2)]
        s_filled, s_read = sem("s_filled"), sem("s_read")
        pv_done, o_copied = sem("pv_done"), sem("o_copied")
        o_normed, oT_ready, mid_ready = sem("o_normed"), sem("oT_ready"), sem("mid_ready")
        logits_shifted, logits_exped, gates_ready = sem("logits_shifted"), sem("logits_exped"), sem("gates_ready")
        gateT_ready, bias_added = sem("gateT_ready"), sem("bias_added")
        combined = sem("combined")
        stored = sem("stored")

        norms = {}
        for step in PLAN:
            if step[0] in ("hat", "ctx_hat"):
                norms[step if step[0] == "hat" else "ctx_hat"] = len(norms)

        def phase_input(p):
            return (x_sb, x_mid, x_out)[p // 2][:, p % 2]

        block = ctx.enter_context(nc.Block())

        def k_on_dve(b):
            return b == 0

        def neg_on_dve(g):
            return g == 0 or g >= 8

        def split_maxima(eng, link, g, waiter):
            if g:
                waiter.wait_ge(misc_filled, MISC_USE[("mT", g - 1)] + 1)
            link(eng.tensor_scalar(neg_full[:, :], row_max[:, g], -1.0, None, ALU.mult))
            link(eng.tensor_copy(neg_part[:, 0], neg_full[:, :]))
            link(eng.tensor_tensor(neg_rest[:, :], neg_full[:, :], neg_part[:, 0], ALU.subtract))
            link(eng.tensor_copy(neg_part[:, 1], neg_rest[:, :]))
            eng.tensor_tensor(neg_part[:, 2], neg_rest[:, :], neg_part[:, 1], ALU.subtract).then_inc(neg_split, 1)

        @block.sync
        def _(sp):
            tokens = x.rearrange("b (t p) d -> b p t d", p=P)
            sp.dma_start(x_sb[:, 0], tokens[0]).then_inc(x_loaded[0], 16)
            sp.dma_start(cols_sb[:, :], cols).then_inc(cols_loaded, 16)
            sp.dma_start(w_in_sb[:, :, :], w_in).then_inc(w_in_loaded, 16)
            sp.dma_start(x_sb[:, 1], tokens[1]).then_inc(x_loaded[1], 16)
            sp.dma_start(ctx_sb[:, :, 0, :], ctx_in[:, 0:P, :].rearrange("b p d -> p b d")).then_inc(ctx_loaded, 16)
            sp.dma_start(ctx_sb[0:TB, :, 1, :], ctx_in[:, P:T, :].rearrange("b p d -> p b d")).then_inc(ctx_loaded, 16)
            sp.dma_start(rows_sb[:, :], rows.partition_broadcast(P)).then_inc(rows_loaded, 16)
            sp.dma_start(w_out_sb[:, :, :], w_out).then_inc(w_out_loaded, 16)
            sp.dma_start(fc2_b_sb[:, :], fc2_b).then_inc(fc2_b_loaded, 16)
            for step in PLAN:
                kind, n = step[0], step[-1]
                if kind == "q":
                    sp.wait_ge(q_low, n + 1)
                    sp.wait_ge(tiles_cleared[n % 2], 2)
                    for r, part in enumerate(Q_PARTS):
                        sp.dma_start(q_tile[DH * r:DH * r + DH, n % 2], q_part[:, part, :]).then_inc(q_moved[n], 16)
                elif kind == "k":
                    sp.wait_ge(ones_ready, 1)
                    for quarter in range(4):
                        sp.dma_start(k_tile[SELF_MAX_ROW:SELF_MAX_ROW + 3, n, 4 * quarter:4 * quarter + 4, :],
                                     ones_row[:, :]).then_inc(key_ones[n], 16)
                    sp.wait_ge(k_low, n + 1)
                    for r, part in enumerate(K_PARTS):
                        sp.dma_start(k_tile[DH * r:DH * r + DH, n], k_part[:, part, :]).then_inc(k_moved[n], 16)
                elif kind == "ctx_k":
                    sp.wait_ge(ctx_cleared, 1)
                    for b in range(B):
                        for half in range(2):
                            sp.dma_start(kc_tile[CROSS_MAX_ROW:CROSS_MAX_ROW + 3, b, 8 * half:8 * half + 8, :],
                                         ones_row[:, 0:8 * TP]).then_inc(ctx_key_ones, 16)
                    sp.wait_ge(k_low, B + 1)
                    for b in range(B):
                        for r, part in enumerate(K_PARTS):
                            sp.dma_start(kc_tile[DH * r:DH * r + DH, b, :, 0:T],
                                         k_part[:, part, b * T:b * T + T]).then_inc(kc_moved, 16)
                elif kind == "mT":
                    sp.wait_ge(neg_turned, n + 1)
                    b, g = n // G % B, n % G
                    row = SELF_MAX_ROW if n < B * G else CROSS_MAX_ROW
                    sp.dma_start(q_tile[row:row + 3, b, 4 * g:4 * g + 4, :],
                                 neg_rows[:, n % 2]).then_inc(neg_moved[n % 2], 16)
                elif kind == "load_fc1":
                    sp.wait_ge(s_filled, S_RING["scores", SELF_UNITS - 1] + 1)
                    sp.dma_start(fc1_sb, fc1_w).then_inc(fc1_loaded, 16)
                elif kind == "load_fc2":
                    sp.wait_ge(s_filled, S_RING["scores", 2 * SELF_UNITS - 1] + 1)
                    sp.dma_start(fc2_sb, fc2_w).then_inc(fc2_loaded, 16)
                elif kind == "store":
                    sp.wait_ge(combined, E * (n + 1))
                    sp.dma_start(out[n].rearrange("(t p) d -> p t d", p=P), x_out[:, n]).then_inc(stored, 16)
            sp.wait_ge(stored, 16 * B)

        @block.gpsimd
        def _(pool):
            steps = [0]

            def link(ins):
                steps[0] += 1
                ins.then_inc(pool_chain, 1)
                pool.wait_ge(pool_chain, steps[0])

            link(nc.gpsimd.memset(ident[:, :], 0.0))
            nc.gpsimd.affine_select(out=ident[:, :], in_=ident[:, :], compare_op=ALU.not_equal, fill=1.0, base=0,
                                    pattern=[[-1, P]], channel_multiplier=1).then_inc(ident_ready, 1)
            link(nc.gpsimd.memset(power[:, :], -0.5))
            pool.wait_ge(ident_ready, 1)
            nc.gpsimd.tensor_copy(ident_bf[:, :], ident[:, :]).then_inc(ident_ready, 1)

            def clear_values(b):
                nc.gpsimd.memset(v_aug[:, b, :, :, DH + 1:], 0.0).then_inc(v_cleared, 1)
                nc.gpsimd.memset(v_aug[:, b, :, :, DH:DH + 1], 1.0).then_inc(v_cleared, 1)

            def clear_first():
                nc.gpsimd.memset(ones_row[:, :], 1.0).then_inc(ones_ready, 1)
                clear_values(0)

            def clear_rest():
                nc.gpsimd.memset(q_tile[:, 1].bitcast(F32), 0.0).then_inc(tiles_cleared[1], 1)
                nc.gpsimd.memset(k_tile[:, 1].bitcast(F32), 0.0).then_inc(tiles_cleared[1], 1)
                clear_values(1)
                nc.gpsimd.memset(kc_tile[:, :, :, :].bitcast(F32), 0.0).then_inc(ctx_cleared, 1)
                nc.gpsimd.memset(vc_aug[:, :, :, DH + 1:], 0.0).then_inc(ctx_cleared, 1)
                nc.gpsimd.memset(vc_aug[:, :, :, DH:DH + 1], 1.0).then_inc(ctx_cleared, 1)
                link(nc.gpsimd.memset(vc_diag[:, :, :, :, :], 0.0))
                for j in range(4):
                    nc.gpsimd.memset(vc_diag[32 * j:32 * j + TB, :, :, j, DH:DH + 1], 1.0).then_inc(ctx_cleared, 1)
                    pool.wait_ge(ctx_cleared, 4 + j)
                link(nc.gpsimd.memset(lower[:, :, :], 1.0))
                nc.gpsimd.affine_select(out=lower[:, :, :], in_=lower[:, :, :], compare_op=ALU.is_gt, fill=0.0,
                                        base=0, pattern=[[1, E], [-1, E]], channel_multiplier=0) \
                    .then_inc(lower_ready, 1)

            def k_split(n, width, moved):
                pool.wait_ge(k_high, n)
                pool.wait_ge(*moved)
                link(nc.gpsimd.tensor_tensor(k_rest[:, 0:width], k_full[:, 0:width], k_part[:, 0, 0:width], ALU.subtract))
                link(nc.gpsimd.tensor_copy(k_part[:, 1, 0:width], k_rest[:, 0:width]))
                nc.gpsimd.tensor_tensor(k_part[:, 2, 0:width], k_rest[:, 0:width], k_part[:, 1, 0:width],
                                        ALU.subtract).then_inc(k_low, 1)
                pool.wait_ge(k_low, n + 1)

            def inverse_std(out_, var, eps_out, size):
                link(nc.gpsimd.tensor_scalar(eps_out, var, EPS, None, ALU.add))
                return nc.gpsimd.tensor_tensor(out_, eps_out, power[0:size, 0:out_.shape[1]], ALU.pow)

            for step in PLAN:
                if step[0] == "k" and k_on_dve(step[1]):
                    clear_rest()
                elif step[0] == "ln":
                    pool.wait_ge(var_ready, norms["hat", step[1]] + 1)
                    inverse_std(rstd[:, :], mean_var[:, :, 1], var_eps[:, :], P).then_inc(rstd_ready, 1)
                    if step[1] == 0:
                        clear_first()
                elif step[0] == "ctx_ln":
                    pool.wait_ge(var_ready, norms["ctx_hat"] + 1)
                    link(inverse_std(c_rstd[:, :, 0], c_mean_var[:, :, 0, 1], var_eps[:, 0:B], P))
                    inverse_std(c_rstd[0:TB, :, 1], c_mean_var[0:TB, :, 1, 1], var_eps[0:TB, 0:B], TB) \
                        .then_inc(rstd_ready, 1)
                elif step[0] == "k":
                    b = step[1]
                    k_split(b, S, (k_moved[0], 16 * len(K_PARTS)))
                elif step[0] == "ctx_k":
                    k_split(B, B * T, (k_moved[1], 16 * len(K_PARTS)))
                elif step[0] == "neg" and not neg_on_dve(step[1]):
                    pool.wait_ge(m_read, M_RING["max", last_max(step[1])] + 1)
                    split_maxima(nc.gpsimd, link, step[1], pool)

        @block.scalar
        def _(act):
            def col(c, n=P):
                return cols_sb[0:n, c:c + 1]

            act.wait_ge(zero_ready, 1)
            nc.scalar.activation(q_tile[:, 0].bitcast(F32).rearrange("p h s -> p (h s)"),
                                 zero[:, :].to_broadcast([P, H * S // 2]), ACT.Identity) \
                .then_inc(tiles_cleared[0], 1)
            for step in PLAN:
                kind, n = step[0], step[-1]
                if step in MISC_USE and kind not in ("oT", "proj", "router", "b2", "ctx_vB"):
                    act.wait_ge(misc_filled, MISC_USE[step] + 1)
                if kind == "hT":
                    g = (C_SA_G, C_CQ_G, C_MO_G)[n // 2]
                    act.wait_ge(cols_loaded, 16)
                    nc.scalar.activation(hT[:, n % 2], ps_x[:, :], ACT.Identity, bias=col(g + 1), scale=col(g)) \
                        .then_inc(misc_read, 1)
                elif kind == "q":
                    bias = col(C_SA_BQ if n < 2 else C_CA_BQ)
                    if n:
                        act.wait_ge(q_moved[n - 1], 16 * len(Q_PARTS))
                    nc.scalar.activation(q_part[:, 0], ps_x[:, :], ACT.Identity, bias=bias).then_inc(q_high, 1)
                elif kind == "ctx_k" or kind == "k" and not k_on_dve(n):
                    m, width = (n, S) if kind == "k" else (2, B * T)
                    bias = col(C_SA_BK if kind == "k" else C_CA_BK)
                    act.wait_ge(k_moved[m - 1], 16 * len(K_PARTS))
                    act.wait_ge(k_low, m)
                    nc.scalar.activation(k_part[:, 0, 0:width], ps_x[:, 0:width], ACT.Identity, bias=bias)
                    nc.scalar.activation(k_full[:, 0:width], ps_x[:, 0:width], ACT.Identity, bias=bias) \
                        .then_inc(k_high, 1)
                    act.wait_ge(k_high, m)
                    act.sem_inc(misc_read, 1)
                elif kind == "v":
                    nc.scalar.activation(v_aug[:, n, :, :, 0:DH],
                                         ps_x[:, :].rearrange("p (c h d) -> p c h d", c=QT, d=DH),
                                         ACT.Identity).then_inc(misc_read, 1)
                elif kind == "ctx_T":
                    nc.scalar.activation(ctxT[:, :], ps_x[:, 0:B * T], ACT.Identity, bias=col(C_KV_B),
                                         scale=col(C_KV_G)).then_inc(misc_read, 1)
                elif kind == "ctx_vA":
                    nc.scalar.activation(vc_aug[:, :, :, 0:DH],
                                         ps_x[:, 0:B * D].rearrange("p (b h d) -> p b h d", b=B, d=DH),
                                         ACT.Identity).then_inc(misc_read, 1)
                elif kind == "mT":
                    if n >= 2:
                        act.wait_ge(neg_moved[n % 2], 16 * (n // 2))
                    nc.scalar.activation(neg_rows[:, n % 2], ps_x[0:48, 0:P // 2].bitcast(BF16),
                                         ACT.Identity).then_inc(neg_turned, 1)
                    act.wait_ge(neg_turned, n + 1)
                    act.sem_inc(misc_read, 1)
                elif kind == "scores":
                    for m in pieces_of(n):
                        r = S_RING["scores", m]
                        act.wait_ge(s_filled, r + 1)
                        if quad(m) >= 2:
                            act.wait_ge(pv_done, quad(m) - 1)
                        nc.scalar.activation(probs[:, probs_slot(m)], ps_s[:, r % 3], ACT.Exp,
                                             scale=SCALE).then_inc(s_read, 1)
                elif kind == "pv" and (n >= 16 or n % 2):
                    g = n // 2 if n < 16 else n - 8
                    act.wait_ge(pv_done, n + 1)
                    if g >= 2:
                        act.wait_ge(misc_filled, MISC_USE[("oT", g - 2)] + 1)
                    nc.scalar.activation(o_raw[:, g % 2], ps_o[:, :], ACT.Identity).then_inc(o_copied, 1)
                elif kind == "osT":
                    nc.scalar.activation(oT[:, :], ps_x[:, :], ACT.Identity,
                                         bias=col(C_SA_BV if n < 2 else C_CA_BV)).then_inc(misc_read, 1)
                elif kind == "gates":
                    act.wait_ge(logits_shifted, n + 1)
                    nc.scalar.activation(expd[:, :, :], shifted[:, :, :], ACT.Exp).then_inc(logits_exped, 1)
                elif kind == "gT":
                    nc.scalar.activation(gateT[:, :], ps_x[0:E, :], ACT.Identity).then_inc(misc_read, 1)
                elif kind == "fc1":
                    for c in range(FC):
                        r = S_RING["fc1", FC * n + c]
                        act.wait_ge(s_filled, r + 1)
                        if n >= 2 and c == 0:
                            act.wait_ge(m_filled, M_RING["fc2", n - 2] + 1)
                        nc.scalar.activation(hidden[:, FC * (n % 2) + c], ps_s[:, r % 3], ACT.Gelu,
                                             bias=col(C_FC1_B + FC * (n % E) + c)).then_inc(s_read, 1)

        @block.vector
        def _(dve):
            steps = [0]

            def link(ins):
                steps[0] += 1
                ins.then_inc(dve_chain, 1)
                dve.wait_ge(dve_chain, steps[0])

            nc.vector.memset(zero[:, :], 0.0).then_inc(zero_ready, 1)
            nc.vector.memset(k_tile[:, 0].bitcast(F32), 0.0).then_inc(tiles_cleared[0], 1)

            for step in PLAN:
                kind, n = step[0], step[-1]
                if kind in ("oT", "proj", "router", "b2", "ctx_vB"):
                    dve.wait_ge(misc_filled, MISC_USE[step] + 1)
                if kind == "ln":
                    src = phase_input(n)
                    if n < 2:
                        dve.wait_ge(x_loaded[n], 16)
                    else:
                        dve.wait_ge(mid_ready, n - 1)
                        dve.wait_ge(misc_filled, MISC_USE[("hT", n - 1)] + 1)
                    if n == 1:
                        dve.wait_ge(misc_filled, MISC_USE[("hT", 0)] + 1)
                    for t in range(QT):
                        ins = nc.vector.bn_stats(stats[:, t], src[:, t])
                    link(ins)
                    for t in range(QT):
                        ins = nc.vector.bn_aggr(mean_var[:, t], stats[:, t])
                    ins.then_inc(var_ready, 1)
                elif kind == "hat":
                    src = phase_input(n)
                    dve.wait_ge(rstd_ready, norms["hat", n] + 1)
                    for t in range(QT):
                        ins = nc.vector.tensor_scalar(x_hat[:, t], src[:, t], mean_var[:, t, 0:1], rstd[:, t:t + 1],
                                                      ALU.subtract, ALU.mult)
                    ins.then_inc(hat_ready, 1)
                elif kind == "ctx_ln":
                    dve.wait_ge(ctx_loaded, 32)
                    for c, size in ((0, P), (1, TB)):
                        for b in range(B):
                            ins = nc.vector.bn_stats(c_stats[0:size, b, c], ctx_sb[0:size, b, c])
                    link(ins)
                    for c, size in ((0, P), (1, TB)):
                        for b in range(B):
                            ins = nc.vector.bn_aggr(c_mean_var[0:size, b, c], c_stats[0:size, b, c])
                    ins.then_inc(var_ready, 1)
                elif kind == "ctx_hat":
                    dve.wait_ge(rstd_ready, norms["ctx_hat"] + 1)
                    for c, size in ((0, P), (1, TB)):
                        for b in range(B):
                            ins = nc.vector.tensor_scalar(c_hat[0:size, b, c], ctx_sb[0:size, b, c],
                                                          c_mean_var[0:size, b, c, 0:1], c_rstd[0:size, b, c:c + 1],
                                                          ALU.subtract, ALU.mult)
                    ins.then_inc(ctx_hat_ready, 1)
                elif kind == "k" and k_on_dve(n):
                    dve.wait_ge(k0_filled, 1)
                    dve.wait_ge(cols_loaded, 16)
                    bias = cols_sb[:, C_SA_BK:C_SA_BK + 1]
                    link(nc.vector.tensor_scalar(k_part[:, 0], ps_o[:, :], bias, None, ALU.add))
                    link(nc.vector.scalar_tensor_tensor(out=k_rest[:, :], in0=ps_o[:, :], scalar=bias,
                                                        in1=k_part[:, 0], op0=ALU.add, op1=ALU.subtract))
                    link(nc.vector.tensor_copy(k_part[:, 1], k_rest[:, :]))
                    nc.vector.tensor_tensor(k_part[:, 2], k_rest[:, :], k_part[:, 1], ALU.subtract).then_inc(k_low, 1)
                elif kind == "neg" and neg_on_dve(n):
                    dve.wait_ge(m_read, M_RING["max", last_max(n)] + 1)
                    split_maxima(nc.vector, link, n, dve)
                elif kind == "q":
                    c_bias = C_SA_BQ if n < 2 else C_CA_BQ
                    dve.wait_ge(q_high, n + 1)
                    link(nc.vector.scalar_tensor_tensor(
                        out=q_rest[:, :], in0=ps_x[:, :], scalar=cols_sb[:, c_bias:c_bias + 1], in1=q_part[:, 0],
                        op0=ALU.add, op1=ALU.subtract))
                    dve.sem_inc(misc_read, 1)
                    link(nc.vector.tensor_copy(q_part[:, 1], q_rest[:, :]))
                    nc.vector.tensor_tensor(q_part[:, 2], q_rest[:, :], q_part[:, 1], ALU.subtract).then_inc(q_low, 1)
                elif kind == "ctx_vB":
                    dve.wait_ge(ctx_cleared, 7)
                    for b in range(B):
                        for j in range(4):
                            rows_j = slice(32 * j, 32 * j + TB)
                            src = ps_x[rows_j, b * D:b * D + D].rearrange("p (g j d) -> p g j d", g=G, j=4)[:, :, j]
                            ins = nc.vector.tensor_copy(vc_diag[rows_j, b, :, j, 0:DH], src)
                    ins.then_inc(misc_read, 1)
                elif kind == "max":
                    r = M_RING[step]
                    dve.wait_ge(m_filled, r + 1)
                    if n < SELF_MAX:
                        nc.vector.tensor_reduce(row_max[:, n // 16, n % 16:n % 16 + 1], ps_m[:, r % 3], AX.X,
                                                ALU.max).then_inc(m_read, 1)
                    else:
                        c, i = (n - SELF_MAX) // 8, (n - SELF_MAX) % 8
                        t, pair = i // 2, i % 2
                        dst = row_max[:, 8 + c].rearrange("p (h t) -> p h t", t=QT)[:, 2 * pair:2 * pair + 2, t]
                        nc.vector.tensor_reduce(dst, ps_m[:, r % 3, 0:2 * T].rearrange("p (h k) -> p h k", k=T),
                                                AX.X, ALU.max).then_inc(m_read, 1)
                elif kind == "oT":
                    raw = ps_x[:, :].rearrange("p (t j c) -> p t j c", t=QT, j=4)
                    b, g = n // G % B, n % G
                    link(nc.vector.reciprocal(o_rden[:, :, :], raw[:, :, :, DH]))
                    ins = nc.vector.tensor_tensor(o_tok[:, b, :, 4 * g:4 * g + 4, :], raw[:, :, :, 0:DH],
                                                  o_rden[:, :, :].unsqueeze(3).to_broadcast([P, QT, 4, DH]), ALU.mult)
                    ins.then_inc(misc_read, 1)
                    dve.wait_ge(misc_read, MISC_USE[step] + 1)
                    if g == G - 1:
                        dve.sem_inc(o_normed, 1)
                elif kind == "proj":
                    b = n % B
                    src, dst = (x_sb, x_mid) if n < 2 else (x_mid, x_out)
                    row = R_SA_OUT if n < 2 else R_CA_OUT
                    dve.wait_ge(rows_loaded, 16)
                    link(nc.vector.tensor_tensor(dst[:, b], src[:, b],
                                                 rows_sb[:, row:row + D].unsqueeze(1).to_broadcast([P, QT, D]), ALU.add))
                    nc.vector.tensor_tensor(dst[:, b], ps_x[:, :].rearrange("p (t d) -> p t d", t=QT), dst[:, b],
                                            ALU.add).then_inc(misc_read, 1)
                    dve.wait_ge(misc_read, MISC_USE[step] + 1)
                    dve.sem_inc(mid_ready, 1)
                elif kind == "router":
                    link(nc.vector.tensor_tensor(logit[:, :, :], ps_x[:, 0:QT * E].rearrange("p (t e) -> p t e", t=QT),
                                                 rows_sb[:, R_ROUTER:R_ROUTER + E].unsqueeze(1)
                                                 .to_broadcast([P, QT, E]), ALU.add))
                    dve.sem_inc(misc_read, 1)
                    link(nc.vector.tensor_reduce(top[:, :], logit[:, :, :], AX.X, ALU.max))
                    nc.vector.tensor_tensor(shifted[:, :, :], logit[:, :, :],
                                            top[:, :].unsqueeze(2).to_broadcast([P, QT, E]),
                                            ALU.subtract).then_inc(logits_shifted, 1)
                elif kind == "gates":
                    dve.wait_ge(lower_ready, 1)
                    for t in range(QT):
                        own = logit[:, t].unsqueeze(2).to_broadcast([P, E, E])
                        other = logit[:, t].unsqueeze(1).to_broadcast([P, E, E])
                        nc.vector.tensor_tensor(beats[:, :, :], other, own, ALU.is_gt)
                        link(nc.vector.tensor_tensor(ties[:, :, :], other, own, ALU.is_equal))
                        link(nc.vector.tensor_tensor(ties[:, :, :], ties[:, :, :], lower[:, :, :], ALU.mult))
                        link(nc.vector.tensor_tensor(beats[:, :, :], beats[:, :, :], ties[:, :, :], ALU.add))
                        link(nc.vector.tensor_reduce(rank[:, t], beats[:, :, :], AX.X, ALU.add))
                    dve.wait_ge(logits_exped, n + 1)
                    link(nc.vector.scalar_tensor_tensor(out=kept[:, :, :], in0=rank[:, :, :], scalar=2.0,
                                                        in1=expd[:, :, :], op0=ALU.is_lt, op1=ALU.mult))
                    link(nc.vector.tensor_reduce(gsum[:, :], kept[:, :, :], AX.X, ALU.add))
                    link(nc.vector.reciprocal(grec[:, :], gsum[:, :]))
                    nc.vector.tensor_tensor(gate[:, n], kept[:, :, :], grec[:, :].unsqueeze(2)
                                            .to_broadcast([P, QT, E]), ALU.mult).then_inc(gates_ready, 1)
                elif kind == "b2":
                    nc.vector.tensor_tensor(x_out[:, n], ps_x[:, :].rearrange("p (t d) -> p t d", t=QT), x_out[:, n],
                                            ALU.add).then_inc(misc_read, 1)
                elif kind == "fc2":
                    b, e, r = n // E, n % E, M_RING[step]
                    dve.wait_ge(m_filled, r + 1)
                    if e == 0:
                        dve.wait_ge(misc_read, MISC_USE[("b2", b)] + 1)
                    for t in range(QT):
                        ins = nc.vector.scalar_tensor_tensor(out=x_out[:, b, t], in0=ps_m[:, r % 3, t * D:t * D + D],
                                                             scalar=gate[:, b, t, e:e + 1], in1=x_out[:, b, t],
                                                             op0=ALU.mult, op1=ALU.add)
                    ins.then_inc(combined, 1)
                    dve.wait_ge(combined, n + 1)
                    dve.sem_inc(m_read, 1)

        @block.tensor
        def _(pe):
            pe.wait_ge(ident_ready, 1)

            def transposes(src, cols_of, rows_in=P):
                for t in range(QT):
                    mm = nc.tensor.transpose(ps_x[0:cols_of, t * P:t * P + rows_in], src(t), ident[0:rows_in, 0:rows_in])
                return mm

            for step in PLAN:
                kind, n = step[0], step[-1]
                if step == ("k", 0):
                    pe.wait_ge(w_in_loaded, 16)
                    pe.wait_ge(misc_read, MISC_USE[("hT", 0)] + 1)
                    nc.tensor.matmul(ps_o[:, :], w_in_sb[:, 0, D:2 * D], hT[:, 0], start=True, stop=True) \
                        .then_inc(k0_filled, 1)
                    continue
                if MISC_USE.get(step):
                    pe.wait_ge(misc_read, MISC_USE[step])
                mm = None
                if kind == "hT":
                    pe.wait_ge(hat_ready, n + 1)
                    mm = transposes(lambda t: x_hat[:, t], P)
                elif kind == "q":
                    a = 0 if n < 2 else 1
                    pe.wait_ge(w_in_loaded, 16)
                    pe.wait_ge(misc_read, MISC_USE[("hT", n)] + 1)
                    mm = nc.tensor.matmul(ps_x[:, :], w_in_sb[:, a, 0:D], hT[:, n % 2], start=True, stop=True)
                elif kind == "k":
                    mm = nc.tensor.matmul(ps_x[:, :], w_in_sb[:, 0, D:2 * D], hT[:, n], start=True, stop=True)
                elif kind == "v":
                    for c in range(QT):
                        mm = nc.tensor.matmul(ps_x[:, c * D:c * D + D], hT[:, n, c * P:c * P + P],
                                              w_in_sb[:, 0, 2 * D:3 * D], start=True, stop=True)
                elif kind == "ctx_T":
                    pe.wait_ge(ctx_hat_ready, 1)
                    for b in range(B):
                        nc.tensor.transpose(ps_x[:, b * T:b * T + P], c_hat[:, b, 0], ident[:, :])
                        mm = nc.tensor.transpose(ps_x[:, b * T + P:b * T + T], c_hat[0:TB, b, 1], ident[0:TB, 0:TB])
                elif kind == "ctx_k":
                    mm = nc.tensor.matmul(ps_x[:, 0:B * T], w_in_sb[:, 1, D:2 * D], ctxT[:, :], start=True, stop=True)
                elif kind == "ctx_vA":
                    for b in range(B):
                        mm = nc.tensor.matmul(ps_x[:, b * D:b * D + D], ctxT[:, b * T:b * T + P],
                                              w_in_sb[:, 1, 2 * D:3 * D], start=True, stop=True)
                elif kind == "ctx_vB":
                    for b in range(B):
                        for j in range(4):
                            mm = nc.tensor.matmul(ps_x[32 * j:32 * j + TB, b * D:b * D + D],
                                                  ctxT[:, b * T + P:b * T + T], w_in_sb[:, 1, 2 * D:3 * D],
                                                  start=True, stop=True, tile_position=(0, 32 * j))
                elif kind == "max":
                    r = M_RING[step]
                    if r >= 3:
                        pe.wait_ge(m_read, r - 2)
                    if n < SELF_MAX:
                        b, h, t = n // 64, n % 64 // 4, n % 4
                        if n % 64 == 0:
                            pe.wait_ge(q_moved[b], 16 * len(Q_PARTS))
                            pe.wait_ge(k_moved[b], 16 * len(K_PARTS))
                            pe.wait_ge(key_ones[b], 16 * 4)
                        mm = nc.tensor.matmul(ps_m[:, r % 3], q_tile[:, b, h, t * P:t * P + P], k_tile[:, b, h],
                                              start=True, stop=True)
                    else:
                        c, i = (n - SELF_MAX) // 8, (n - SELF_MAX) % 8
                        b, t, pair = c // G, i // 2, i % 2
                        if c % G == 0 and i == 0:
                            pe.wait_ge(q_moved[2 + b], 16 * len(Q_PARTS))
                            pe.wait_ge(kc_moved, 16 * B * len(K_PARTS))
                            pe.wait_ge(ctx_key_ones, 16 * 4)
                        for k in range(2):
                            h = 4 * (c % G) + 2 * pair + k
                            mm = nc.tensor.matmul(ps_m[:, r % 3, k * T:k * T + T], q_tile[:, b, h, t * P:t * P + P],
                                                  kc_tile[:, b, h, 0:T], start=True, stop=True)
                    mm.then_inc(m_filled, 1)
                    mm = None
                elif kind == "mT":
                    pe.wait_ge(ident_ready, 2)
                    pe.wait_ge(neg_split, n + 1)
                    mm = nc.tensor.transpose(ps_x[0:48, 0:P // 2].bitcast(BF16),
                                             neg_part[:, :, :].rearrange("p s n -> p (s n)"), ident_bf[:, :])
                elif kind == "scores":
                    g = group_of(n)
                    pe.wait_ge(neg_moved[g % 2], 16 * (g // 2 + 1))
                    for k, m in enumerate(pieces_of(n)):
                        r = S_RING["scores", m]
                        if r >= 3:
                            pe.wait_ge(s_read, r - 2)
                        if n < SELF_UNITS:
                            b, h, c = n // 32, 4 * (n // 8 % G) + n % 4, 2 * (n % 8 // 4) + k
                            mm = nc.tensor.matmul(ps_s[:, r % 3], k_tile[:, b, h, c * P:c * P + P], q_tile[:, b, h],
                                                  start=True, stop=True)
                        else:
                            c, i = (n - SELF_UNITS) // 3, (n - SELF_UNITS) % 3
                            b, h0 = c // G, 4 * (c % G)
                            if i < 2:
                                h = h0 + 2 * i + k
                                mm = nc.tensor.matmul(ps_s[:, r % 3], kc_tile[:, b, h, 0:P], q_tile[:, b, h],
                                                      start=True, stop=True)
                            else:
                                for j in range(4):
                                    mm = nc.tensor.matmul(ps_s[32 * j:32 * j + 32, r % 3], kc_tile[:, b, h0 + j, P:TP],
                                                          q_tile[:, b, h0 + j], start=True, stop=True,
                                                          tile_position=(0, 32 * j))
                        mm.then_inc(s_filled, 1)
                    mm = None
                elif kind == "pv":
                    pe.wait_ge(s_read, S_RING["scores", last_piece(n)] + 1)
                    if n < 16:
                        b, g, half = n // 8, n // 2 % G, n % 2
                        if half == 0 and n:
                            pe.wait_ge(o_copied, n // 2)
                        if n % 8 == 0:
                            pe.wait_ge(misc_read, MISC_USE[("v", b)] + 1)
                            pe.wait_ge(v_cleared, 2 * (b + 1))
                        for k in range(2):
                            for j in range(4):
                                mm = nc.tensor.matmul(ps_o[32 * j:32 * j + 32, :], v_aug[:, b, 2 * half + k, 4 * g + j],
                                                      probs[:, probs_slot(8 * n + 2 * j + k)],
                                                      start=(half == 0 and k == 0), stop=(half == 1 and k == 1),
                                                      tile_position=(0, 32 * j), skip_group_check=True)
                    else:
                        c = n - 16
                        b, g = c // G, c % G
                        pe.wait_ge(o_copied, n - 8)
                        if c == 0:
                            pe.wait_ge(misc_read, MISC_USE[("ctx_vB",)] + 1)
                            pe.wait_ge(ctx_cleared, 7)
                        nc.tensor.matmul(ps_o[:, :], vc_diag[:, b, g].rearrange("p j c -> p (j c)"),
                                         probs[:, probs_slot(2 * SELF_UNITS + 5 * c + 4)],
                                         start=True, stop=False, skip_group_check=True)
                        for j in range(4):
                            mm = nc.tensor.matmul(ps_o[32 * j:32 * j + 32, :], vc_aug[:, b, 4 * g + j],
                                                  probs[:, probs_slot(2 * SELF_UNITS + 5 * c + j)],
                                                  start=False, stop=True, tile_position=(0, 32 * j),
                                                  skip_group_check=True)
                    mm.then_inc(pv_done, 1)
                    mm = None
                elif kind == "oT":
                    pe.wait_ge(o_copied, n + 1)
                    mm = transposes(lambda t: o_raw[:, n % 2, t * P:t * P + P], P)
                elif kind == "osT":
                    pe.wait_ge(o_normed, n + 1)
                    mm = transposes(lambda t: o_tok[:, n % 2, t].rearrange("p h d -> p (h d)"), P)
                elif kind == "proj":
                    pe.wait_ge(w_out_loaded, 16)
                    pe.wait_ge(misc_read, MISC_USE[("osT", n)] + 1)
                    for t in range(QT):
                        mm = nc.tensor.matmul(ps_x[:, t * D:t * D + D], oT[:, t * P:t * P + P], w_out_sb[:, n // 2],
                                              start=True, stop=True)
                elif kind == "router":
                    pe.wait_ge(misc_read, MISC_USE[("hT", 4 + n)] + 1)
                    for t in range(QT):
                        mm = nc.tensor.matmul(ps_x[:, t * E:t * E + E], hT[:, n, t * P:t * P + P],
                                              cols_sb[:, C_ROUTER:C_ROUTER + E], start=True, stop=True)
                elif kind == "gT":
                    pe.wait_ge(gates_ready, n + 1)
                    mm = transposes(lambda t: gate[:, n, t], E)
                elif kind == "b2":
                    pe.wait_ge(fc2_b_loaded, 16)
                    pe.wait_ge(misc_read, MISC_USE[("gT", n)] + 1)
                    for t in range(QT):
                        mm = nc.tensor.matmul(ps_x[:, t * D:t * D + D], gateT[:, t * P:t * P + P], fc2_b_sb[:, :],
                                              start=True, stop=True)
                elif kind == "fc1":
                    b, e = n // E, n % E
                    if n == 0:
                        pe.wait_ge(fc1_loaded, 16)
                    if e == 0:
                        pe.wait_ge(misc_read, MISC_USE[("hT", 4 + b)] + 1)
                    for c in range(FC):
                        r = S_RING["fc1", FC * n + c]
                        pe.wait_ge(s_read, r - 2)
                        nc.tensor.matmul(ps_s[:, r % 3], fc1_sb[:, e, c * P:c * P + P], hT[:, b],
                                         start=True, stop=True).then_inc(s_filled, 1)
                elif kind == "fc2":
                    b, e = n // E, n % E
                    if n == 0:
                        pe.wait_ge(fc2_loaded, 16)
                    r = M_RING[step]
                    pe.wait_ge(s_read, S_RING["fc1", FC * n + FC - 1] + 1)
                    pe.wait_ge(m_read, r - 2)
                    for t in range(QT):
                        for c in range(FC):
                            mm = nc.tensor.matmul(ps_m[:, r % 3, t * D:t * D + D],
                                                  hidden[:, FC * (n % 2) + c, t * P:t * P + P], fc2_sb[:, e, c],
                                                  start=(c == 0), stop=(c == FC - 1))
                    mm.then_inc(m_filled, 1)
                    mm = None
                if mm is not None:
                    mm.then_inc(misc_filled, 1)


def kernel(x, ctx_1024, L0_xattn_sa_ln_g, L0_xattn_sa_ln_b, L0_xattn_sa_in_w, L0_xattn_sa_in_b, L0_xattn_sa_out_w,
           L0_xattn_sa_out_b, L0_xattn_ca_q_ln_g, L0_xattn_ca_q_ln_b, L0_xattn_ca_kv_ln_g, L0_xattn_ca_kv_ln_b,
           L0_xattn_ca_in_w, L0_xattn_ca_in_b, L0_xattn_ca_out_w, L0_xattn_ca_out_b, L0_xattn_moe_ln_g,
           L0_xattn_moe_ln_b, L0_xattn_router_w, L0_xattn_router_b, L0_xattn_e_fc1_w, L0_xattn_e_fc1_b,
           L0_xattn_e_fc2_w, L0_xattn_e_fc2_b):
    import numpy as np
    import concourse.bacc as bacc
    from concourse import mybir as mb
    from concourse.bass_utils import run_bass_kernel_spmd

    def head_minor(a):
        return np.asarray(a).reshape(H, DH, -1).transpose(1, 0, 2).reshape(D, -1)

    def w_in(a):
        a = np.asarray(a)
        return np.concatenate([head_minor(a[0:D]), head_minor(a[D:2 * D]), a[2 * D:]], axis=0).T

    def b_in(a):
        a = np.asarray(a)
        return [head_minor(a[0:D])[:, 0], head_minor(a[D:2 * D])[:, 0], a[2 * D:]]

    cols = np.stack([np.asarray(a) for a in (
        L0_xattn_sa_ln_g, L0_xattn_sa_ln_b, L0_xattn_ca_q_ln_g, L0_xattn_ca_q_ln_b, L0_xattn_ca_kv_ln_g,
        L0_xattn_ca_kv_ln_b, L0_xattn_moe_ln_g, L0_xattn_moe_ln_b, *b_in(L0_xattn_sa_in_b), *b_in(L0_xattn_ca_in_b))]
        + [a for a in np.asarray(L0_xattn_e_fc1_b).reshape(E * FC, P)]
        + [a for a in np.asarray(L0_xattn_router_w)], axis=1)
    rows = np.concatenate([np.asarray(L0_xattn_sa_out_b), np.asarray(L0_xattn_ca_out_b),
                           np.asarray(L0_xattn_router_b)])
    arrays = {
        "x": np.asarray(x),
        "ctx_in": np.asarray(ctx_1024),
        "w_in": np.stack([w_in(L0_xattn_sa_in_w), w_in(L0_xattn_ca_in_w)], axis=1),
        "w_out": np.stack([np.asarray(L0_xattn_sa_out_w).T, np.asarray(L0_xattn_ca_out_w).T], axis=1),
        "cols": cols,
        "rows": rows,
        "fc1_w": np.asarray(L0_xattn_e_fc1_w).transpose(2, 0, 1),
        "fc2_w": np.asarray(L0_xattn_e_fc2_w).reshape(E, D, FC, P).transpose(3, 0, 2, 1),
        "fc2_b": np.asarray(L0_xattn_e_fc2_b),
    }
    arrays = {k: np.ascontiguousarray(a) for k, a in arrays.items()}
    nc = bacc.Bacc("TRN2", target_bir_lowering=False, num_devices=1)
    args = [nc.dram_tensor(k, a.shape, mb.dt.from_np(a.dtype), kind="ExternalInput").ap() for k, a in arrays.items()]
    out = nc.dram_tensor("out", (B, S, D), F32, kind="ExternalOutput").ap()
    build(nc, *args, out)
    result = run_bass_kernel_spmd(nc, [arrays], core_ids=[0])
    return result.results[0]["out"]
```

```python
from contextlib import ExitStack

import concourse.bass as bass
from concourse import mybir

F32 = mybir.dt.float32
F32R = mybir.dt.float32r
BF16 = mybir.dt.bfloat16
U32 = mybir.dt.uint32
HIGH_BITS = 0xFFFFF000
ALU = mybir.AluOpType
ACT = mybir.ActivationFunctionType
AX = mybir.AxisListType

P = 128
B, S, D = 2, 512, 128
T = 154
H, DH = 16, 8
E, FF = 8, 512
EPS = 1e-5
QT = S // P
FC = FF // P
TB = T - P
TP = 160
G = H // 4
SCALE = float(DH) ** -0.5

Q_PARTS = (0, 0, 1, 1, 0, 2)
K_PARTS = (0, 1, 0, 1, 2, 0)
SELF_MAX_ROW = DH * len(Q_PARTS)
CROSS_MAX_ROW = SELF_MAX_ROW + 3

(C_SA_G, C_SA_B, C_CQ_G, C_CQ_B, C_KV_G, C_KV_B, C_MO_G, C_MO_B,
 C_SA_BQ, C_SA_BK, C_SA_BV, C_CA_BQ, C_CA_BK, C_CA_BV) = range(14)
C_FC1_B = 14
C_ROUTER = C_FC1_B + E * FC
N_COLS = C_ROUTER + E
R_SA_OUT, R_CA_OUT, R_ROUTER = 0, D, 2 * D
N_ROWS = 2 * D + E

SELF_UNITS = B * H * 2
SELF_MAX = B * H * QT
WARM_UP = 42
BANKS = 6
FC2_FIRST = 6


ORDER_OF_STEPS = """
    ln:0 hat:0 hT:0 k:0 q:0 v:0 ln:1 max:0-18 neg:0 max:19-20 hat:1 mT:0 max:21-25 hT:1
    scores:0 max:26 scores:1 max:27-28 scores:2 max:29-31 neg:1 scores:3-5 ctx_ln max:32-36 mT:1 scores:6 q:1
    max:37-38 pv:0 ctx_hat max:39 scores:7 max:40 k:1 max:41-42 scores:8 pv:1 max:43 scores:9 max:44-45 scores:10
    ctx_T max:46 scores:11 max:47 neg:2 max:48-50 v:1 scores:12 max:51-53 mT:2 pv:2 max:54 scores:13 max:55-57
    scores:14 ctx_k max:58-59 scores:15 max:60-61 ctx_vA max:62 scores:16 max:63 scores:17 oT:0 neg:3 scores:18-19
    max:64 pv:3 max:65 scores:20 max:66 mT:3 scores:21 max:67-68 pv:4 scores:22 max:69-70 scores:23 max:71 ctx_vB
    max:72-74 pv:5 max:75 scores:24 max:76 scores:25 max:77-78 scores:26 max:79 neg:4 max:80 scores:27 max:81 oT:1
    scores:28 max:82-84 scores:29 mT:4 max:85 pv:6 max:86 scores:30 max:87-88 scores:31 max:89-90 oT:2 scores:32
    max:91-93 pv:7 max:94 scores:33 max:95 neg:5 oT:3 scores:34 max:96 scores:35 max:97-98 osT:0 max:99 scores:36
    max:100-101 mT:5 scores:37 max:102-103 load_fc1 max:104 proj:0 max:105 ln:2 scores:38-39 max:106 pv:8 scores:40
    max:107 scores:41 max:108 hat:2 max:109-110 pv:9 max:111 scores:42 max:112 hT:2 max:113-114 scores:43 max:115
    neg:6 mT:6 max:116-118 q:2 scores:44-45 max:119 pv:10 scores:46 max:120-121 scores:47 max:122 scores:48 max:123
    oT:4 max:124-127 scores:49 pv:11 max:128-129 scores:50 max:130-133 scores:51 neg:7 mT:7 max:134-136 scores:52
    max:137-138 scores:53 max:139-141 scores:54 max:142-143 scores:55 max:144-145 neg:8 mT:8 max:146-148 pv:12
    max:149 neg:9 mT:9 max:150-154 pv:13 max:155 load_fc2:0 oT:5 max:156 scores:67 max:157-158 neg:10 mT:10 max:159
    scores:68 oT:6 scores:69 scores:64-66 neg:11 mT:11 pv:17 scores:70-72 oT:9 pv:16 scores:73-75 pv:18 scores:56
    oT:8 pv:19 oT:10 scores:57 oT:11 osT:2 scores:58 proj:2 scores:59-60 ln:4 scores:61-62 hat:4 scores:63
    load_fc2:1 pv:14 hT:4 rows_split:0 router:0 fc1_split:0 pv:15 oT:7 gates:0
    fc1:0-1 osT:1 fc1:2-3 proj:1 fc1_split:1 fc2_half:0 ln:3 gT:0 fc1:4 b2:0 hat:3 fc1_split:2 fc2:0 hT:3 fc1:5-6
    q:3 fc1_split:3 fc1:7 fc1_split:4 fc1:8-9 fc2_half:1 fc1:10-12 fc2:1 fc1:13 max:160-167 neg:12 max:168 fc1:14
    max:169 fc1:15 max:170-175 fc2_half:2 fc2:2 max:176 mT:12 fc1:16 max:177-178 fc1:17 max:179-181 fc1:18
    max:182-184 fc1:19 neg:13 mT:13 max:185-187 scores:76 max:188 fc2_half:3 fc1_split:5 scores:77-78 neg:14 mT:14
    fc1_split:6 scores:79 fc2:3 pv:20 max:189-190 scores:80-81 max:191 scores:82 oT:12 fc1:20-21 pv:21 neg:15 mT:15
    fc1:22 scores:83 fc2_half:4 scores:84 oT:13 fc1:23 fc2:4 scores:85 pv:22 scores:86-87 fc2_half:5 oT:14 pv:23
    fc1_split:7 fc1:24-25 oT:15 fc2:5 osT:3 fc1:26-27 proj:3 fc1:28 ln:5 fc1_split:8 fc2_half:6 fc1:29 hat:5 fc2:6
    hT:5 rows_split:1 fc1:30-31 fc1_split:9 router:1 gates:1 fc2_half:7 fc1:32-33 fc2:7 fc1:34-35 fc1_split:10
    fc1:36 gT:1 fc1:37-41 fc2_half:8 b2:1 store:0 fc2:8 fc1_split:11 fc2_half:9 fc2:9 fc1:42-44 fc1_split:12
    fc1:45-46 fc1_split:13 fc2_half:10 fc1:47 fc2:10 fc1:48-49 fc2_half:11 fc2:11 fc1:50-52 fc1_split:14-15
    fc1:53-54 fc2_half:12 fc1:55 fc2:12 fc1:56-58 fc2_half:13 fc1:59-60 fc2:13 fc1:61 fc2_half:14 fc1:62-63 fc2:14
    fc2_half:15 fc2:15 store:1
"""


def make_plan():
    plan = []
    for word in ORDER_OF_STEPS.split():
        kind, _, numbers = word.partition(":")
        if numbers:
            first, _, last = numbers.partition("-")
            plan.extend((kind, n) for n in range(int(first), int(last or first) + 1))
        else:
            plan.append((kind,))
    return plan


PLAN = make_plan()
MISC_KINDS = ("hT", "q", "k", "v", "ctx_T", "ctx_k", "ctx_vA", "ctx_vB", "mT", "oT", "osT", "proj", "router", "gT", "b2")
MISC_USE = {step: n for n, step in enumerate(s for s in PLAN if s[0] in MISC_KINDS and s != ("k", 0))}
ORDER = {step: sum(s[0] == step[0] for s in PLAN[:n]) for n, step in enumerate(PLAN)}


def rows_of(parts, part):
    return [r for r, p in enumerate(parts) if p == part]


EARLY_PARTS = (0, 2)
EARLY = sum(len(rows_of(Q_PARTS, part)) for part in EARLY_PARTS)


def pieces_of(u):
    if u < SELF_UNITS:
        return range(2 * u, 2 * u + 2)
    c, i = (u - SELF_UNITS) // 3, (u - SELF_UNITS) % 3
    first = 2 * SELF_UNITS + 5 * c + 2 * i
    return range(first, first + (2 if i < 2 else 1))


def probs_slot(m):
    return 8 * (ORDER["pv", quad(m)] % 2) + (m % 8 if m < 2 * SELF_UNITS else (m - 2 * SELF_UNITS) % 5)


def quad(m):
    return m // 8 if m < 2 * SELF_UNITS else SELF_UNITS // 4 + (m - 2 * SELF_UNITS) // 5


def last_piece(q):
    return 8 * q + 7 if q < SELF_UNITS // 4 else 2 * SELF_UNITS + 5 * (q - SELF_UNITS // 4) + 4


def last_max(g):
    return 16 * g + 15 if g < 8 else SELF_MAX + 8 * (g - 8) + 7


def number_banks():
    s_ring, m_ring, ring = {}, {}, []

    def use(numbers, key, reader):
        ring.append((reader, len(numbers)))
        numbers[key] = len(numbers)

    for kind, n in (step for step in PLAN if len(step) == 2):
        if kind == "scores":
            for m in pieces_of(n):
                use(s_ring, ("scores", m), "s")
        elif kind == "fc1":
            use(s_ring, ("fc1", n), "s")
        elif kind == "max":
            use(m_ring, ("max", n), "m")
        elif kind == "fc2_half":
            use(m_ring, ("fc2", n), "m")
    return s_ring, m_ring, ring


S_RING, M_RING, RING = number_banks()
RING_PLACE = {use: n for n, use in enumerate(RING)}


def bank(reader, r):
    return RING_PLACE[reader, r] % BANKS


def group_of(w):
    return w // 8 if w < SELF_UNITS else 8 + (w - SELF_UNITS) // 3


def build(nc, x, ctx_in, w_in, w_out, cols, rows, fc1_w, fc2_w, fc2_b, out):
    ctx = ExitStack()
    with ctx:
        def sb(name, shape, dt=F32):
            return ctx.enter_context(nc.sbuf_tensor(name, shape, dt))

        def sem(name):
            return ctx.enter_context(nc.semaphore(name))

        x_sb = sb("x_sb", [P, B, QT, D])
        ctx_sb = sb("ctx_sb", [P, B, 2, D])
        w_in_sb = sb("w_in_sb", [P, 2, 3 * D])
        w_out_sb = sb("w_out_sb", [P, 2, D])
        cols_sb = sb("cols_sb", [P, N_COLS])
        rows_sb = sb("rows_sb", [P, N_ROWS])
        fc2_b_sb = sb("fc2_b_sb", [E, D])
        ident = sb("ident", [P, P])
        ones_row = sb("ones_row", [3, S], BF16)
        power = sb("power", [P, QT])
        zero = sb("zero", [P, 1])
        lower = sb("lower", [P, E, E])
        q_tile = sb("q_tile", [P, B, H, S], BF16)
        k_tile = sb("k_tile", [P, B, H, S], BF16)
        fc1_sb = k_tile[:, 0].bitcast(F32).rearrange("p (e a) n -> p e (a n)", e=E)
        fc2_sb = k_tile[:, 1].bitcast(F32).rearrange("p (e a) n -> p e (a n)", e=E) \
            .rearrange("p e (c d) -> p e c d", c=FC)
        kc_tile = sb("kc_tile", [P, B, H, TP], BF16)
        v_aug = sb("v_aug", [P, B, QT, H, 32])
        hidden = v_aug[:, :, :, :, :].rearrange("p b c h w -> p (b c) (h w)")
        vc_aug = sb("vc_aug", [P, B, H, 32])
        vc_diag = sb("vc_diag", [P, B, G, 4, 32])
        probs = sb("probs", [P, 16, 512])
        q_rest = sb("q_rest", [P, S])
        q_part = sb("q_part", [P, 3, S], BF16)
        k_full, k_rest = sb("k_full", [P, S]), sb("k_rest", [P, S])
        k_part = sb("k_part", [P, 3, S], BF16)
        row_max = sb("row_max", [P, 16, 16])
        neg_full, neg_rest = sb("neg_full", [P, 16]), sb("neg_rest", [P, 16])
        neg_part = sb("neg_part", [P, 3, 16], BF16)
        neg_rows = sb("neg_rows", [48, 2, P], BF16)
        ident_bf = sb("ident_bf", [P, P], BF16)
        stats = sb("stats", [P, QT, 6])
        mean_var = sb("mean_var", [P, QT, 2])
        rstd = sb("rstd", [P, QT])
        x_hat = sb("x_hat", [P, QT, D])
        c_stats = sb("c_stats", [P, B, 2, 6])
        c_mean_var = sb("c_mean_var", [P, B, 2, 2])
        c_rstd = sb("c_rstd", [P, B, 2])
        var_eps = sb("var_eps", [P, QT])
        c_hat = sb("c_hat", [P, B, 2, D])
        hT = sb("hT", [P, 2, S])
        ctxT = sb("ctxT", [P, B * T])
        o_raw = sb("o_raw", [P, 2, S])
        o_rden = sb("o_rden", [P, QT, 4])
        o_tok = sb("o_tok", [P, 2, QT, H, DH])
        oT = sb("oT", [P, S])
        q_full = oT
        x_mid = sb("x_mid", [P, B, QT, D])
        x_out = sb("x_out", [P, B, QT, D])
        logit = sb("logit", [P, QT, E])
        beats = sb("beats", [P, QT, E, E])
        ties = sb("ties", [P, QT, E, E])
        rank = sb("rank", [P, QT, E])
        top = sb("top", [P, QT])
        shifted = sb("shifted", [P, QT, E])
        expd = sb("expd", [P, QT, E])
        kept = sb("kept", [P, QT, E])
        gsum = sb("gsum", [P, QT])
        grec = sb("grec", [P, QT])
        gate = sb("gate", [P, B, QT, E])
        gateT = sb("gateT", [E, S])

        rows_high, rows_low = sb("rows_high", [P, B, S], F32R), sb("rows_low", [P, B, S], F32R)
        fc1_high, fc1_low = sb("fc1_high", [P, 2, FF], F32R), sb("fc1_low", [P, 2, FF], F32R)
        masked = k_full

        ps_r = ctx.enter_context(nc.psum_tensor("ps_r", [P, BANKS, 512], F32))
        ps_o = ctx.enter_context(nc.psum_tensor("ps_o", [P, 512], F32))
        ps_x = ctx.enter_context(nc.psum_tensor("ps_x", [P, 512], F32))

        x_loaded = [sem(f"x_loaded{b}") for b in range(B)]
        ctx_loaded, w_in_loaded, w_out_loaded = sem("ctx_loaded"), sem("w_in_loaded"), sem("w_out_loaded")
        cols_loaded, rows_loaded = sem("cols_loaded"), sem("rows_loaded")
        fc1_loaded, fc2_b_loaded = sem("fc1_loaded"), sem("fc2_b_loaded")
        fc2_loaded = [sem(f"fc2_loaded{i}") for i in range(2)]
        zero_ready = sem("zero_ready")
        ident_ready, ones_ready, lower_ready = sem("ident_ready"), sem("ones_ready"), sem("lower_ready")
        tiles_cleared = [sem(f"tiles_cleared{b}") for b in range(B)]
        ctx_cleared, v_cleared = sem("ctx_cleared"), sem("v_cleared")
        k0_filled = sem("k0_filled")
        key_ones = [sem(f"key_ones{b}") for b in range(B)]
        ctx_key_ones = sem("ctx_key_ones")
        pool_chain = sem("pool_chain")
        dve_chain = sem("dve_chain")
        misc_filled = sem("misc_filled")
        misc_read = sem("misc_read")
        var_ready = sem("var_ready")
        rstd_ready = sem("rstd_ready")
        hat_ready = sem("hat_ready")
        ctx_hat_ready = sem("ctx_hat_ready")
        q_high = sem("q_high")
        q_low = sem("q_low")
        k_high, k_low = sem("k_high"), sem("k_low")
        k0_part = sem("k0_part")
        q_moved = [sem(f"q_moved{p}") for p in range(4)]
        q0_moved_early = sem("q0_moved_early")
        k_moved = [sem(f"k_moved{b}") for b in range(B)]
        kc_moved = sem("kc_moved")
        m_filled, m_read = sem("m_filled"), sem("m_read")
        neg_split, neg_turned = sem("neg_split"), sem("neg_turned")
        neg_moved = [sem(f"neg_moved{i}") for i in range(2)]
        s_filled, s_read = sem("s_filled"), sem("s_read")
        pv_done, o_copied = sem("pv_done"), sem("o_copied")
        o_normed, mid_ready = sem("o_normed"), sem("mid_ready")
        logits_shifted, logits_exped, gates_ready = sem("logits_shifted"), sem("logits_exped"), sem("gates_ready")
        base_ready = sem("base_ready")
        rows_split, fc1_split = sem("rows_split"), sem("fc1_split")
        combined = sem("combined")
        stored = sem("stored")

        norms = {}
        for step in PLAN:
            if step[0] in ("hat", "ctx_hat"):
                norms[step if step[0] == "hat" else "ctx_hat"] = len(norms)

        turned = [MISC_USE[step] for step in PLAN if step[0] == "oT"]
        hats_turned = [MISC_USE[step] for step in PLAN if step[0] == "hT"]

        first_max = [next(s for s in PLAN if s[0] == "max" and lo <= s[1] < lo + size)
                     for lo, size in ((0, 64), (64, 64), (SELF_MAX, 32), (SELF_MAX + 32, 32))]

        def phase_input(p):
            return (x_sb, x_mid, x_out)[p // 2][:, p % 2]

        block = ctx.enter_context(nc.Block())

        def k_on_dve(b):
            return b == 0

        def clearings(b):
            return 3 if b == 0 else 2

        def q_on_pool(p):
            return p == 1

        def q_moves(p):
            return 16 * (len(Q_PARTS) - (EARLY if p == 0 else 0))

        def neg_on_dve(g):
            return g == 0

        def split_maxima(eng, link, g, waiter):
            if g:
                waiter.wait_ge(misc_filled, MISC_USE[("mT", g - 1)] + 1)
            link(eng.tensor_scalar(neg_full[:, :], row_max[:, g], -1.0, None, ALU.mult))
            link(eng.tensor_copy(neg_part[:, 0], neg_full[:, :]))
            link(eng.tensor_tensor(neg_rest[:, :], neg_full[:, :], neg_part[:, 0], ALU.subtract))
            link(eng.tensor_copy(neg_part[:, 1], neg_rest[:, :]))
            eng.tensor_tensor(neg_part[:, 2], neg_rest[:, :], neg_part[:, 1], ALU.subtract).then_inc(neg_split, 1)

        @block.sync
        def _(sp):
            tokens = x.rearrange("b (t p) d -> b p t d", p=P)
            sp.dma_start(x_sb[:, 0], tokens[0]).then_inc(x_loaded[0], 16)
            sp.dma_start(cols_sb[:, :], cols).then_inc(cols_loaded, 16)
            sp.dma_start(w_in_sb[:, :, :], w_in).then_inc(w_in_loaded, 16)
            sp.dma_start(x_sb[:, 1], tokens[1]).then_inc(x_loaded[1], 16)
            sp.dma_start(ctx_sb[:, :, 0, :], ctx_in[:, 0:P, :].rearrange("b p d -> p b d")).then_inc(ctx_loaded, 16)
            sp.dma_start(ctx_sb[0:TB, :, 1, :], ctx_in[:, P:T, :].rearrange("b p d -> p b d")).then_inc(ctx_loaded, 16)
            sp.dma_start(rows_sb[:, :], rows.partition_broadcast(P)).then_inc(rows_loaded, 16)
            sp.dma_start(w_out_sb[:, :, :], w_out).then_inc(w_out_loaded, 16)
            sp.dma_start(fc2_b_sb[:, :], fc2_b).then_inc(fc2_b_loaded, 16)
            for step in PLAN:
                kind, n = step[0], step[-1]
                if kind == "q":
                    sp.wait_ge(q_low, n + 1)
                    sp.wait_ge(tiles_cleared[n % 2], clearings(n % 2))
                    for r, part in enumerate(Q_PARTS):
                        if n == 0 and part in EARLY_PARTS:
                            continue
                        sp.dma_start(q_tile[DH * r:DH * r + DH, n % 2], q_part[:, part, :]).then_inc(q_moved[n], 16)
                elif kind == "k":
                    sp.wait_ge(ones_ready, 1)
                    sp.wait_ge(tiles_cleared[n], clearings(n))
                    sp.dma_start(k_tile[SELF_MAX_ROW:SELF_MAX_ROW + 3, n],
                                 ones_row[:, :].unsqueeze(1).to_broadcast([3, H, S])).then_inc(key_ones[n], 16)
                    if n == 0:
                        for part in range(3):
                            sp.wait_ge(k0_part, part + 1)
                            for r in rows_of(K_PARTS, part):
                                sp.dma_start(k_tile[DH * r:DH * r + DH, n], k_part[:, part, :]).then_inc(k_moved[n], 16)
                        continue
                    sp.wait_ge(k_low, n + 1)
                    for r, part in enumerate(K_PARTS):
                        sp.dma_start(k_tile[DH * r:DH * r + DH, n], k_part[:, part, :]).then_inc(k_moved[n], 16)
                elif kind == "ctx_k":
                    sp.wait_ge(ctx_cleared, 1)
                    sp.dma_start(kc_tile[CROSS_MAX_ROW:CROSS_MAX_ROW + 3, :, :, :],
                                 ones_row[:, 0:TP].unsqueeze(1).to_broadcast([3, B * H, TP])) \
                        .then_inc(ctx_key_ones, 16)
                    sp.wait_ge(k_low, B + 1)
                    for b in range(B):
                        for r, part in enumerate(K_PARTS):
                            sp.dma_start(kc_tile[DH * r:DH * r + DH, b, :, 0:T],
                                         k_part[:, part, b * T:b * T + T]).then_inc(kc_moved, 16)
                elif kind == "mT":
                    sp.wait_ge(neg_turned, n + 1)
                    b, g = n // G % B, n % G
                    row = SELF_MAX_ROW if n < B * G else CROSS_MAX_ROW
                    sp.dma_start(q_tile[row:row + 3, b, 4 * g:4 * g + 4, :],
                                 neg_rows[:, n % 2]).then_inc(neg_moved[n % 2], 16)
                elif kind == "load_fc1":
                    sp.wait_ge(s_filled, S_RING["scores", SELF_UNITS - 1] + 1)
                    sp.dma_start(fc1_sb, fc1_w).then_inc(fc1_loaded, 16)
                elif kind == "load_fc2":
                    sp.wait_ge(s_filled, S_RING["scores", 2 * (SELF_UNITS - 8 if n == 0 else SELF_UNITS) - 1] + 1)
                    experts = slice(0, FC2_FIRST) if n == 0 else slice(FC2_FIRST, E)
                    sp.dma_start(fc2_sb[:, experts], fc2_w[:, experts]).then_inc(fc2_loaded[n], 16)
                elif kind == "store":
                    sp.wait_ge(combined, E * (n + 1))
                    sp.dma_start(out[n].rearrange("(t p) d -> p t d", p=P), x_out[:, n]).then_inc(stored, 16)
            sp.wait_ge(stored, 16 * B)

        @block.gpsimd
        def _(pool):
            steps = [0]

            def link(ins):
                steps[0] += 1
                ins.then_inc(pool_chain, 1)
                pool.wait_ge(pool_chain, steps[0])

            link(nc.gpsimd.memset(ident[:, :], 0.0))
            nc.gpsimd.affine_select(out=ident[:, :], in_=ident[:, :], compare_op=ALU.not_equal, fill=1.0, base=0,
                                    pattern=[[-1, P]], channel_multiplier=1).then_inc(ident_ready, 1)
            link(nc.gpsimd.memset(power[:, :], -0.5))
            pool.wait_ge(ident_ready, 1)
            nc.gpsimd.tensor_copy(ident_bf[:, :], ident[:, :]).then_inc(ident_ready, 1)

            def clear_values(b):
                nc.gpsimd.memset(v_aug[:, b, :, :, DH + 1:], 0.0).then_inc(v_cleared, 1)
                nc.gpsimd.memset(v_aug[:, b, :, :, DH:DH + 1], 1.0).then_inc(v_cleared, 1)

            def clear_first():
                nc.gpsimd.memset(ones_row[:, :], 1.0).then_inc(ones_ready, 1)
                clear_values(0)

            def clear_rest():
                nc.gpsimd.memset(q_tile[:, 1].bitcast(F32), 0.0).then_inc(tiles_cleared[1], 1)
                pool.wait_ge(q_high, 1)
                pool.wait_ge(tiles_cleared[0], clearings(0))
                for part in EARLY_PARTS:
                    if part:
                        pool.wait_ge(q_low, 1)
                    for r in rows_of(Q_PARTS, part):
                        nc.gpsimd.dma_start(q_tile[DH * r:DH * r + DH, 0], q_part[:, part, :]) \
                            .then_inc(q0_moved_early, 16)
                nc.gpsimd.memset(k_tile[:, 1].bitcast(F32), 0.0).then_inc(tiles_cleared[1], 1)
                clear_values(1)
                nc.gpsimd.memset(kc_tile[:, :, :, :].bitcast(F32), 0.0).then_inc(ctx_cleared, 1)
                nc.gpsimd.memset(vc_aug[:, :, :, DH + 1:], 0.0).then_inc(ctx_cleared, 1)
                nc.gpsimd.memset(vc_aug[:, :, :, DH:DH + 1], 1.0).then_inc(ctx_cleared, 1)
                link(nc.gpsimd.memset(vc_diag[:, :, :, :, :], 0.0))
                for j in range(4):
                    nc.gpsimd.memset(vc_diag[32 * j:32 * j + TB, :, :, j, DH:DH + 1], 1.0).then_inc(ctx_cleared, 1)
                    pool.wait_ge(ctx_cleared, 4 + j)
                link(nc.gpsimd.memset(lower[:, :, :], 1.0))
                nc.gpsimd.affine_select(out=lower[:, :, :], in_=lower[:, :, :], compare_op=ALU.is_gt, fill=0.0,
                                        base=0, pattern=[[1, E], [-1, E]], channel_multiplier=0) \
                    .then_inc(lower_ready, 1)

            def k_split(n, width, moved):
                pool.wait_ge(k_high, n)
                pool.wait_ge(*moved)
                link(nc.gpsimd.tensor_tensor(k_rest[:, 0:width], k_full[:, 0:width], k_part[:, 0, 0:width],
                                             ALU.subtract))
                link(nc.gpsimd.tensor_copy(k_part[:, 1, 0:width], k_rest[:, 0:width]))
                nc.gpsimd.tensor_tensor(k_part[:, 2, 0:width], k_rest[:, 0:width], k_part[:, 1, 0:width],
                                        ALU.subtract).then_inc(k_low, 1)
                pool.wait_ge(k_low, n + 1)

            def inverse_std(out_, var, eps_out, size):
                link(nc.gpsimd.tensor_scalar(eps_out, var, EPS, None, ALU.add))
                return nc.gpsimd.tensor_tensor(out_, eps_out, power[0:size, 0:out_.shape[1]], ALU.pow)

            for step in PLAN:
                if step[0] == "k" and k_on_dve(step[1]):
                    clear_rest()
                elif step[0] == "ln":
                    pool.wait_ge(var_ready, norms["hat", step[1]] + 1)
                    inverse_std(rstd[:, :], mean_var[:, :, 1], var_eps[:, :], P).then_inc(rstd_ready, 1)
                    if step[1] == 0:
                        clear_first()
                elif step[0] == "ctx_ln":
                    pool.wait_ge(var_ready, norms["ctx_hat"] + 1)
                    link(inverse_std(c_rstd[:, :, 0], c_mean_var[:, :, 0, 1], var_eps[:, 0:B], P))
                    inverse_std(c_rstd[0:TB, :, 1], c_mean_var[0:TB, :, 1, 1], var_eps[0:TB, 0:B], TB) \
                        .then_inc(rstd_ready, 1)
                elif step[0] == "k":
                    b = step[1]
                    k_split(b, S, (k_moved[0], 16 * len(K_PARTS)))
                elif step[0] == "ctx_k":
                    k_split(B, B * T, (k_moved[1], 16 * len(K_PARTS)))
                elif step[0] == "q" and q_on_pool(step[1]):
                    pool.wait_ge(q_high, step[1] + 1)
                    link(nc.gpsimd.tensor_tensor(q_rest[:, :], q_full[:, :], q_part[:, 0], ALU.subtract))
                    link(nc.gpsimd.tensor_copy(q_part[:, 1], q_rest[:, :]))
                    nc.gpsimd.tensor_tensor(q_part[:, 2], q_rest[:, :], q_part[:, 1], ALU.subtract).then_inc(q_low, 1)
                elif step[0] == "osT":
                    n, b = step[1], step[1] % B
                    src, dst, row = (x_sb, x_mid, R_SA_OUT) if n < 2 else (x_mid, x_out, R_CA_OUT)
                    if n < 2:
                        pool.wait_ge(x_loaded[b], 16)
                    else:
                        pool.wait_ge(mid_ready, ORDER["proj", n - 2] + 1)
                    pool.wait_ge(rows_loaded, 16)
                    nc.gpsimd.tensor_tensor(dst[:, b], src[:, b],
                                            rows_sb[:, row:row + D].unsqueeze(1).to_broadcast([P, QT, D]),
                                            ALU.add).then_inc(base_ready, 1)
                elif step[0] == "neg" and not neg_on_dve(step[1]):
                    pool.wait_ge(m_read, M_RING["max", last_max(step[1])] + 1)
                    split_maxima(nc.gpsimd, link, step[1], pool)

        @block.scalar
        def _(act):
            def col(c, n=P):
                return cols_sb[0:n, c:c + 1]

            act.wait_ge(zero_ready, 1)
            nc.scalar.activation(q_tile[:, 0].bitcast(F32).rearrange("p h s -> p (h s)"),
                                 zero[:, :].to_broadcast([P, H * S // 2]), ACT.Identity) \
                .then_inc(tiles_cleared[0], 1)
            nc.scalar.activation(k_tile[:, 0, 0:H // 2].bitcast(F32).rearrange("p h s -> p (h s)"),
                                 zero[:, :].to_broadcast([P, H * S // 4]), ACT.Identity) \
                .then_inc(tiles_cleared[0], 1)
            for step in PLAN:
                kind, n = step[0], step[-1]
                if step in MISC_USE and kind not in ("oT", "proj", "router", "b2", "ctx_vB"):
                    act.wait_ge(misc_filled, MISC_USE[step] + 1)
                if kind == "hT":
                    g = (C_SA_G, C_CQ_G, C_MO_G)[n // 2]
                    act.wait_ge(cols_loaded, 16)
                    nc.scalar.activation(hT[:, n % 2], ps_x[:, :], ACT.Identity, bias=col(g + 1), scale=col(g)) \
                        .then_inc(misc_read, 1)
                elif kind == "q":
                    bias = col(C_SA_BQ if n < 2 else C_CA_BQ)
                    if n:
                        act.wait_ge(q_moved[n - 1], q_moves(n - 1))
                    if n == 1:
                        act.wait_ge(q0_moved_early, 16 * EARLY)
                    if q_on_pool(n):
                        nc.scalar.activation(q_part[:, 0], ps_x[:, :], ACT.Identity, bias=bias)
                        nc.scalar.activation(q_full[:, :], ps_x[:, :], ACT.Identity, bias=bias).then_inc(q_high, 1)
                        act.wait_ge(q_high, n + 1)
                        act.sem_inc(misc_read, 1)
                    else:
                        nc.scalar.activation(q_part[:, 0], ps_x[:, :], ACT.Identity, bias=bias).then_inc(q_high, 1)
                elif kind == "ctx_k" or kind == "k" and not k_on_dve(n):
                    m, width = (n, S) if kind == "k" else (2, B * T)
                    bias = col(C_SA_BK if kind == "k" else C_CA_BK)
                    act.wait_ge(k_moved[m - 1], 16 * len(K_PARTS))
                    act.wait_ge(k_low, m)
                    nc.scalar.activation(k_part[:, 0, 0:width], ps_x[:, 0:width], ACT.Identity, bias=bias)
                    nc.scalar.activation(k_full[:, 0:width], ps_x[:, 0:width], ACT.Identity, bias=bias) \
                        .then_inc(k_high, 1)
                    act.wait_ge(k_high, m)
                    act.sem_inc(misc_read, 1)
                elif kind == "v":
                    nc.scalar.activation(v_aug[:, n, :, :, 0:DH],
                                         ps_x[:, :].rearrange("p (c h d) -> p c h d", c=QT, d=DH),
                                         ACT.Identity).then_inc(misc_read, 1)
                elif kind == "ctx_T":
                    nc.scalar.activation(ctxT[:, :], ps_x[:, 0:B * T], ACT.Identity, bias=col(C_KV_B),
                                         scale=col(C_KV_G)).then_inc(misc_read, 1)
                elif kind == "ctx_vA":
                    nc.scalar.activation(vc_aug[:, :, :, 0:DH],
                                         ps_x[:, 0:B * D].rearrange("p (b h d) -> p b h d", b=B, d=DH),
                                         ACT.Identity).then_inc(misc_read, 1)
                elif kind == "mT":
                    if n >= 2:
                        act.wait_ge(neg_moved[n % 2], 16 * (n // 2))
                    nc.scalar.activation(neg_rows[:, n % 2], ps_x[0:48, 0:P // 2].bitcast(BF16),
                                         ACT.Identity).then_inc(neg_turned, 1)
                    act.wait_ge(neg_turned, n + 1)
                    act.sem_inc(misc_read, 1)
                elif kind == "scores":
                    for m in pieces_of(n):
                        r = S_RING["scores", m]
                        act.wait_ge(s_filled, r + 1)
                        if ORDER["pv", quad(m)] >= 2:
                            act.wait_ge(pv_done, ORDER["pv", quad(m)] - 1)
                        nc.scalar.activation(probs[:, probs_slot(m)], ps_r[:, bank("s", r)], ACT.Exp,
                                             scale=SCALE).then_inc(s_read, 1)
                elif kind == "pv" and (n >= 16 or n % 2):
                    o = ORDER["oT", n // 2 if n < 16 else n - 8]
                    act.wait_ge(pv_done, ORDER[step] + 1)
                    if o >= 2:
                        act.wait_ge(misc_filled, turned[o - 2] + 1)
                    nc.scalar.activation(o_raw[:, o % 2], ps_o[:, :], ACT.Identity).then_inc(o_copied, 1)
                elif kind == "osT":
                    nc.scalar.activation(oT[:, :], ps_x[:, :], ACT.Identity,
                                         bias=col(C_SA_BV if n < 2 else C_CA_BV)).then_inc(misc_read, 1)
                elif kind == "gates":
                    act.wait_ge(logits_shifted, n + 1)
                    nc.scalar.activation(expd[:, :, :], shifted[:, :, :], ACT.Exp).then_inc(logits_exped, 1)
                elif kind == "gT":
                    nc.scalar.activation(gateT[:, :], ps_x[0:E, :], ACT.Identity).then_inc(misc_read, 1)
                elif kind == "fc1":
                    r = S_RING[step]
                    act.wait_ge(s_filled, r + 1)
                    if n >= 2 * FC and n % FC == 0:
                        act.wait_ge(m_filled, M_RING["fc2", n // FC - 2] + 1)
                    nc.scalar.activation(hidden[:, n % (2 * FC)], ps_r[:, bank("s", r)], ACT.Gelu,
                                         bias=col(C_FC1_B + n % (E * FC))).then_inc(s_read, 1)

        @block.vector
        def _(dve):
            steps = [0]

            def link(ins):
                steps[0] += 1
                ins.then_inc(dve_chain, 1)
                dve.wait_ge(dve_chain, steps[0])

            def split_in_halves(high, low, full):
                link(nc.vector.tensor_scalar(masked[:, :].bitcast(U32), full.bitcast(U32), HIGH_BITS, None,
                                             ALU.bitwise_and))
                link(nc.vector.tensor_copy(high, masked[:, :]))
                return nc.vector.tensor_tensor(low, full, masked[:, :], ALU.subtract)

            nc.vector.memset(zero[:, :], 0.0).then_inc(zero_ready, 1)

            for step in PLAN:
                kind, n = step[0], step[-1]
                if kind in ("oT", "proj", "router", "b2", "ctx_vB"):
                    dve.wait_ge(misc_filled, MISC_USE[step] + 1)
                if kind == "ln":
                    src = phase_input(n)
                    if n < 2:
                        dve.wait_ge(x_loaded[n], 16)
                    else:
                        dve.wait_ge(mid_ready, ORDER["proj", n - 2] + 1)
                    if n:
                        dve.wait_ge(misc_filled, hats_turned[ORDER[step] - 1] + 1)
                    for t in range(QT):
                        ins = nc.vector.bn_stats(stats[:, t], src[:, t])
                    link(ins)
                    for t in range(QT):
                        ins = nc.vector.bn_aggr(mean_var[:, t], stats[:, t])
                    ins.then_inc(var_ready, 1)
                elif kind == "hat":
                    src = phase_input(n)
                    dve.wait_ge(rstd_ready, norms["hat", n] + 1)
                    for t in range(QT):
                        nc.vector.tensor_scalar(x_hat[:, t], src[:, t], mean_var[:, t, 0:1], rstd[:, t:t + 1],
                                                ALU.subtract, ALU.mult).then_inc(hat_ready, 1)
                    if n == 0:
                        nc.vector.memset(k_tile[:, 0, H // 2:].bitcast(F32), 0.0).then_inc(tiles_cleared[0], 1)
                elif kind == "ctx_ln":
                    dve.wait_ge(ctx_loaded, 32)
                    for c, size in ((0, P), (1, TB)):
                        for b in range(B):
                            ins = nc.vector.bn_stats(c_stats[0:size, b, c], ctx_sb[0:size, b, c])
                    link(ins)
                    for c, size in ((0, P), (1, TB)):
                        for b in range(B):
                            ins = nc.vector.bn_aggr(c_mean_var[0:size, b, c], c_stats[0:size, b, c])
                    ins.then_inc(var_ready, 1)
                elif kind == "ctx_hat":
                    dve.wait_ge(rstd_ready, norms["ctx_hat"] + 1)
                    for c, size in ((0, P), (1, TB)):
                        for b in range(B):
                            ins = nc.vector.tensor_scalar(c_hat[0:size, b, c], ctx_sb[0:size, b, c],
                                                          c_mean_var[0:size, b, c, 0:1], c_rstd[0:size, b, c:c + 1],
                                                          ALU.subtract, ALU.mult)
                    ins.then_inc(ctx_hat_ready, 1)
                elif kind == "k" and k_on_dve(n):
                    dve.wait_ge(k0_filled, 1)
                    dve.wait_ge(cols_loaded, 16)
                    bias = cols_sb[:, C_SA_BK:C_SA_BK + 1]
                    nc.vector.tensor_scalar(k_part[:, 0], ps_o[:, :], bias, None, ALU.add).then_inc(k0_part, 1)
                    dve.wait_ge(k0_part, 1)
                    link(nc.vector.scalar_tensor_tensor(out=k_rest[:, :], in0=ps_o[:, :], scalar=bias,
                                                        in1=k_part[:, 0], op0=ALU.add, op1=ALU.subtract))
                    nc.vector.tensor_copy(k_part[:, 1], k_rest[:, :]).then_inc(k0_part, 1)
                    dve.wait_ge(k0_part, 2)
                    nc.vector.tensor_tensor(k_part[:, 2], k_rest[:, :], k_part[:, 1], ALU.subtract).then_inc(k0_part, 1)
                    dve.wait_ge(k0_part, 3)
                    dve.sem_inc(k_low, 1)
                elif kind == "neg" and neg_on_dve(n):
                    dve.wait_ge(m_read, M_RING["max", last_max(n)] + 1)
                    split_maxima(nc.vector, link, n, dve)
                elif kind == "q" and not q_on_pool(n):
                    c_bias = C_SA_BQ if n < 2 else C_CA_BQ
                    dve.wait_ge(q_high, n + 1)
                    link(nc.vector.scalar_tensor_tensor(
                        out=q_rest[:, :], in0=ps_x[:, :], scalar=cols_sb[:, c_bias:c_bias + 1], in1=q_part[:, 0],
                        op0=ALU.add, op1=ALU.subtract))
                    dve.sem_inc(misc_read, 1)
                    link(nc.vector.tensor_copy(q_part[:, 1], q_rest[:, :]))
                    nc.vector.tensor_tensor(q_part[:, 2], q_rest[:, :], q_part[:, 1], ALU.subtract).then_inc(q_low, 1)
                elif kind == "ctx_vB":
                    dve.wait_ge(ctx_cleared, 7)
                    for b in range(B):
                        for j in range(4):
                            rows_j = slice(32 * j, 32 * j + TB)
                            src = ps_x[rows_j, b * D:b * D + D].rearrange("p (g j d) -> p g j d", g=G, j=4)[:, :, j]
                            ins = nc.vector.tensor_copy(vc_diag[rows_j, b, :, j, 0:DH], src)
                    ins.then_inc(misc_read, 1)
                elif kind == "max":
                    r = M_RING[step]
                    dve.wait_ge(m_filled, r + 1)
                    if n < SELF_MAX:
                        nc.vector.tensor_reduce(row_max[:, n // 16, n % 16:n % 16 + 1], ps_r[:, bank("m", r)], AX.X,
                                                ALU.max).then_inc(m_read, 1)
                    else:
                        c, i = (n - SELF_MAX) // 8, (n - SELF_MAX) % 8
                        t, pair = i // 2, i % 2
                        dst = row_max[:, 8 + c].rearrange("p (h t) -> p h t", t=QT)[:, 2 * pair:2 * pair + 2, t]
                        nc.vector.tensor_reduce(dst, ps_r[:, bank("m", r), 0:2 * T].rearrange("p (h k) -> p h k", k=T),
                                                AX.X, ALU.max).then_inc(m_read, 1)
                elif kind == "oT":
                    raw = ps_x[:, :].rearrange("p (t j c) -> p t j c", t=QT, j=4)
                    b, g = n // G % B, n % G
                    link(nc.vector.reciprocal(o_rden[:, :, :], raw[:, :, :, DH]))
                    ins = nc.vector.tensor_tensor(o_tok[:, b, :, 4 * g:4 * g + 4, :], raw[:, :, :, 0:DH],
                                                  o_rden[:, :, :].unsqueeze(3).to_broadcast([P, QT, 4, DH]), ALU.mult)
                    ins.then_inc(misc_read, 1)
                    dve.wait_ge(misc_read, MISC_USE[step] + 1)
                    if g == G - 1:
                        dve.sem_inc(o_normed, 1)
                elif kind == "proj":
                    b = n % B
                    dst = x_mid if n < 2 else x_out
                    dve.wait_ge(base_ready, ORDER[step] + 1)
                    nc.vector.tensor_tensor(dst[:, b], ps_x[:, :].rearrange("p (t d) -> p t d", t=QT), dst[:, b],
                                            ALU.add).then_inc(misc_read, 1)
                    dve.wait_ge(misc_read, MISC_USE[step] + 1)
                    dve.sem_inc(mid_ready, 1)
                elif kind == "router":
                    link(nc.vector.tensor_tensor(logit[:, :, :], ps_x[:, 0:QT * E].rearrange("p (t e) -> p t e", t=QT),
                                                 rows_sb[:, R_ROUTER:R_ROUTER + E].unsqueeze(1)
                                                 .to_broadcast([P, QT, E]), ALU.add))
                    dve.sem_inc(misc_read, 1)
                    link(nc.vector.tensor_reduce(top[:, :], logit[:, :, :], AX.X, ALU.max))
                    nc.vector.tensor_tensor(shifted[:, :, :], logit[:, :, :],
                                            top[:, :].unsqueeze(2).to_broadcast([P, QT, E]),
                                            ALU.subtract).then_inc(logits_shifted, 1)
                elif kind == "gates":
                    dve.wait_ge(lower_ready, 1)
                    own = logit[:, :, :].unsqueeze(3).to_broadcast([P, QT, E, E])
                    other = logit[:, :, :].unsqueeze(2).to_broadcast([P, QT, E, E])
                    first = lower[:, :, :].unsqueeze(1).to_broadcast([P, QT, E, E])
                    nc.vector.tensor_tensor(beats[:, :, :, :], other, own, ALU.is_gt)
                    link(nc.vector.tensor_tensor(ties[:, :, :, :], other, own, ALU.is_equal))
                    link(nc.vector.tensor_tensor(ties[:, :, :, :], ties[:, :, :, :], first, ALU.mult))
                    link(nc.vector.tensor_tensor(beats[:, :, :, :], beats[:, :, :, :], ties[:, :, :, :], ALU.add))
                    link(nc.vector.tensor_reduce(rank[:, :, :], beats[:, :, :, :], AX.X, ALU.add))
                    dve.wait_ge(logits_exped, n + 1)
                    link(nc.vector.scalar_tensor_tensor(out=kept[:, :, :], in0=rank[:, :, :], scalar=2.0,
                                                        in1=expd[:, :, :], op0=ALU.is_lt, op1=ALU.mult))
                    link(nc.vector.tensor_reduce(gsum[:, :], kept[:, :, :], AX.X, ALU.add))
                    link(nc.vector.reciprocal(grec[:, :], gsum[:, :]))
                    nc.vector.tensor_tensor(gate[:, n], kept[:, :, :], grec[:, :].unsqueeze(2)
                                            .to_broadcast([P, QT, E]), ALU.mult).then_inc(gates_ready, 1)
                elif kind == "b2":
                    nc.vector.tensor_tensor(x_out[:, n], ps_x[:, :].rearrange("p (t d) -> p t d", t=QT), x_out[:, n],
                                            ALU.add).then_inc(misc_read, 1)
                elif kind == "rows_split":
                    dve.wait_ge(misc_read, MISC_USE[("hT", 4 + n)] + 1)
                    split_in_halves(rows_high[:, n], rows_low[:, n], hT[:, n]).then_inc(rows_split, 1)
                    dve.wait_ge(rows_split, n + 1)
                elif kind == "fc1_split":
                    if n == 0:
                        dve.wait_ge(fc1_loaded, 16)
                        dve.wait_ge(k_low, B + 1)
                    if n >= 2:
                        dve.wait_ge(s_filled, S_RING["fc1", FC * (n - 2) + FC - 1] + 1)
                    split_in_halves(fc1_high[:, n % 2], fc1_low[:, n % 2], fc1_sb[:, n % E]).then_inc(fc1_split, 1)
                    dve.wait_ge(fc1_split, n + 1)
                elif kind == "fc2":
                    b, e, r = n // E, n % E, M_RING[step]
                    if e == 0:
                        dve.wait_ge(misc_read, MISC_USE[("b2", b)] + 1)
                    dve.wait_ge(m_filled, r + 1)
                    for t in range(QT):
                        ins = nc.vector.scalar_tensor_tensor(
                            out=x_out[:, b, t], in0=ps_r[:, bank("m", r), t * D:t * D + D],
                            scalar=gate[:, b, t, e:e + 1], in1=x_out[:, b, t], op0=ALU.mult, op1=ALU.add)
                    ins.then_inc(combined, 1)
                    dve.wait_ge(combined, n + 1)
                    dve.sem_inc(m_read, 1)

        @block.tensor
        def _(pe):
            pe.wait_ge(ident_ready, 2)
            for _ in range(WARM_UP):
                nc.tensor.matmul(ps_r[:, 0, 0:P], ident_bf[:, :], ident_bf[:, :], start=True, stop=True)

            def wait_for_bank(reader, r):
                place = RING_PLACE[reader, r]
                if place >= BANKS:
                    last_reader, last = RING[place - BANKS]
                    pe.wait_ge(s_read if last_reader == "s" else m_read, last + 1)

            def transposes(src, cols_of, rows_in=P):
                for t in range(QT):
                    mm = nc.tensor.transpose(ps_x[0:cols_of, t * P:t * P + rows_in], src(t), ident[0:rows_in, 0:rows_in])
                return mm

            for step in PLAN:
                kind, n = step[0], step[-1]
                if step == ("k", 0):
                    pe.wait_ge(w_in_loaded, 16)
                    pe.wait_ge(misc_read, MISC_USE[("hT", 0)] + 1)
                    nc.tensor.matmul(ps_o[:, :], w_in_sb[:, 0, D:2 * D], hT[:, 0], start=True, stop=True) \
                        .then_inc(k0_filled, 1)
                    continue
                if MISC_USE.get(step):
                    pe.wait_ge(misc_read, MISC_USE[step])
                mm = None
                if kind == "hT":
                    for t in range(QT):
                        pe.wait_ge(hat_ready, QT * ORDER[step] + t + 1)
                        mm = nc.tensor.transpose(ps_x[:, t * P:t * P + P], x_hat[:, t], ident[:, :])
                elif kind == "q":
                    a = 0 if n < 2 else 1
                    pe.wait_ge(w_in_loaded, 16)
                    pe.wait_ge(misc_read, MISC_USE[("hT", n)] + 1)
                    mm = nc.tensor.matmul(ps_x[:, :], w_in_sb[:, a, 0:D], hT[:, n % 2], start=True, stop=True)
                elif kind == "k":
                    mm = nc.tensor.matmul(ps_x[:, :], w_in_sb[:, 0, D:2 * D], hT[:, n], start=True, stop=True)
                elif kind == "v":
                    for c in range(QT):
                        mm = nc.tensor.matmul(ps_x[:, c * D:c * D + D], hT[:, n, c * P:c * P + P],
                                              w_in_sb[:, 0, 2 * D:3 * D], start=True, stop=True)
                elif kind == "ctx_T":
                    pe.wait_ge(ctx_hat_ready, 1)
                    for b in range(B):
                        nc.tensor.transpose(ps_x[:, b * T:b * T + P], c_hat[:, b, 0], ident[:, :])
                        mm = nc.tensor.transpose(ps_x[:, b * T + P:b * T + T], c_hat[0:TB, b, 1], ident[0:TB, 0:TB])
                elif kind == "ctx_k":
                    mm = nc.tensor.matmul(ps_x[:, 0:B * T], w_in_sb[:, 1, D:2 * D], ctxT[:, :], start=True, stop=True)
                elif kind == "ctx_vA":
                    for b in range(B):
                        mm = nc.tensor.matmul(ps_x[:, b * D:b * D + D], ctxT[:, b * T:b * T + P],
                                              w_in_sb[:, 1, 2 * D:3 * D], start=True, stop=True)
                elif kind == "ctx_vB":
                    for b in range(B):
                        for j in range(4):
                            mm = nc.tensor.matmul(ps_x[32 * j:32 * j + TB, b * D:b * D + D],
                                                  ctxT[:, b * T + P:b * T + T], w_in_sb[:, 1, 2 * D:3 * D],
                                                  start=True, stop=True, tile_position=(0, 32 * j))
                elif kind == "max":
                    r = M_RING[step]
                    wait_for_bank("m", r)
                    if n < SELF_MAX:
                        b, h, t = n // 64, n % 64 // 4, n % 4
                        if step == first_max[b]:
                            pe.wait_ge(q_moved[b], q_moves(b))
                            if b == 0:
                                pe.wait_ge(q0_moved_early, 16 * EARLY)
                            pe.wait_ge(k_moved[b], 16 * len(K_PARTS))
                            pe.wait_ge(key_ones[b], 16)
                        mm = nc.tensor.matmul(ps_r[:, bank("m", r)], q_tile[:, b, h, t * P:t * P + P], k_tile[:, b, h],
                                              start=True, stop=True)
                    else:
                        c, i = (n - SELF_MAX) // 8, (n - SELF_MAX) % 8
                        b, t, pair = c // G, i // 2, i % 2
                        if step == first_max[2 + b]:
                            pe.wait_ge(q_moved[2 + b], q_moves(2 + b))
                            pe.wait_ge(kc_moved, 16 * B * len(K_PARTS))
                            pe.wait_ge(ctx_key_ones, 16)
                        for k in range(2):
                            h = 4 * (c % G) + 2 * pair + k
                            mm = nc.tensor.matmul(ps_r[:, bank("m", r), k * T:k * T + T], q_tile[:, b, h, t * P:t * P + P],
                                                  kc_tile[:, b, h, 0:T], start=True, stop=True)
                    mm.then_inc(m_filled, 1)
                    mm = None
                elif kind == "mT":
                    pe.wait_ge(ident_ready, 2)
                    pe.wait_ge(neg_split, n + 1)
                    mm = nc.tensor.transpose(ps_x[0:48, 0:P // 2].bitcast(BF16),
                                             neg_part[:, :, :].rearrange("p s n -> p (s n)"), ident_bf[:, :])
                elif kind == "scores":
                    g = group_of(n)
                    pe.wait_ge(neg_moved[g % 2], 16 * (g // 2 + 1))
                    for k, m in enumerate(pieces_of(n)):
                        r = S_RING["scores", m]
                        wait_for_bank("s", r)
                        if n < SELF_UNITS:
                            b, h, c = n // 32, 4 * (n // 8 % G) + n % 4, 2 * (n % 8 // 4) + k
                            mm = nc.tensor.matmul(ps_r[:, bank("s", r)], k_tile[:, b, h, c * P:c * P + P], q_tile[:, b, h],
                                                  start=True, stop=True)
                        else:
                            c, i = (n - SELF_UNITS) // 3, (n - SELF_UNITS) % 3
                            b, h0 = c // G, 4 * (c % G)
                            if i < 2:
                                h = h0 + 2 * i + k
                                mm = nc.tensor.matmul(ps_r[:, bank("s", r)], kc_tile[:, b, h, 0:P], q_tile[:, b, h],
                                                      start=True, stop=True)
                            else:
                                for j in range(4):
                                    mm = nc.tensor.matmul(ps_r[32 * j:32 * j + 32, bank("s", r)], kc_tile[:, b, h0 + j, P:TP],
                                                          q_tile[:, b, h0 + j], start=True, stop=True,
                                                          tile_position=(0, 32 * j))
                        mm.then_inc(s_filled, 1)
                    mm = None
                elif kind == "pv":
                    pe.wait_ge(s_read, S_RING["scores", last_piece(n)] + 1)
                    if n < 16:
                        b, g, half = n // 8, n // 2 % G, n % 2
                        if half == 0 and n:
                            pe.wait_ge(o_copied, ORDER["oT", n // 2])
                        if n % 8 == 0:
                            pe.wait_ge(misc_read, MISC_USE[("v", b)] + 1)
                            pe.wait_ge(v_cleared, 2 * (b + 1))
                        for k in range(2):
                            for j in range(4):
                                mm = nc.tensor.matmul(ps_o[32 * j:32 * j + 32, :], v_aug[:, b, 2 * half + k, 4 * g + j],
                                                      probs[:, probs_slot(8 * n + 2 * j + k)],
                                                      start=(half == 0 and k == 0), stop=(half == 1 and k == 1),
                                                      tile_position=(0, 32 * j), skip_group_check=True)
                    else:
                        c = n - 16
                        b, g = c // G, c % G
                        pe.wait_ge(o_copied, ORDER["oT", n - 8])
                        if c == 0:
                            pe.wait_ge(misc_read, MISC_USE[("ctx_vB",)] + 1)
                            pe.wait_ge(ctx_cleared, 7)
                        nc.tensor.matmul(ps_o[:, :], vc_diag[:, b, g].rearrange("p j c -> p (j c)"),
                                         probs[:, probs_slot(2 * SELF_UNITS + 5 * c + 4)],
                                         start=True, stop=False, skip_group_check=True)
                        for j in range(4):
                            mm = nc.tensor.matmul(ps_o[32 * j:32 * j + 32, :], vc_aug[:, b, 4 * g + j],
                                                  probs[:, probs_slot(2 * SELF_UNITS + 5 * c + j)],
                                                  start=False, stop=True, tile_position=(0, 32 * j),
                                                  skip_group_check=True)
                    mm.then_inc(pv_done, 1)
                    mm = None
                elif kind == "oT":
                    pe.wait_ge(o_copied, ORDER[step] + 1)
                    mm = transposes(lambda t: o_raw[:, ORDER[step] % 2, t * P:t * P + P], P)
                elif kind == "osT":
                    pe.wait_ge(o_normed, ORDER[step] + 1)
                    mm = transposes(lambda t: o_tok[:, n % 2, t].rearrange("p h d -> p (h d)"), P)
                elif kind == "proj":
                    pe.wait_ge(w_out_loaded, 16)
                    pe.wait_ge(misc_read, MISC_USE[("osT", n)] + 1)
                    for t in range(QT):
                        mm = nc.tensor.matmul(ps_x[:, t * D:t * D + D], oT[:, t * P:t * P + P], w_out_sb[:, n // 2],
                                              start=True, stop=True)
                elif kind == "router":
                    pe.wait_ge(misc_read, MISC_USE[("hT", 4 + n)] + 1)
                    for t in range(QT):
                        mm = nc.tensor.matmul(ps_x[:, t * E:t * E + E], hT[:, n, t * P:t * P + P],
                                              cols_sb[:, C_ROUTER:C_ROUTER + E], start=True, stop=True)
                elif kind == "gT":
                    pe.wait_ge(gates_ready, n + 1)
                    mm = transposes(lambda t: gate[:, n, t], E)
                elif kind == "b2":
                    pe.wait_ge(fc2_b_loaded, 16)
                    pe.wait_ge(misc_read, MISC_USE[("gT", n)] + 1)
                    for t in range(QT):
                        mm = nc.tensor.matmul(ps_x[:, t * D:t * D + D], gateT[:, t * P:t * P + P], fc2_b_sb[:, :],
                                              start=True, stop=True)
                elif kind == "fc1":
                    b, e, c = n // FC // E, n // FC % E, n % FC
                    r = S_RING[step]
                    if c == 0:
                        pe.wait_ge(fc1_split, n // FC + 1)
                        if e == 0:
                            pe.wait_ge(rows_split, b + 1)
                    wait_for_bank("s", r)
                    chunk, slot = slice(c * P, c * P + P), n // FC % 2
                    nc.tensor.matmul(ps_r[:, bank("s", r)], fc1_high[:, slot, chunk], rows_high[:, b], start=True, stop=False)
                    nc.tensor.matmul(ps_r[:, bank("s", r)], fc1_high[:, slot, chunk], rows_low[:, b], start=False, stop=False)
                    nc.tensor.matmul(ps_r[:, bank("s", r)], fc1_low[:, slot, chunk], rows_high[:, b],
                                     start=False, stop=True).then_inc(s_filled, 1)
                elif kind in ("fc2_half", "fc2"):
                    e, r = n % E, M_RING["fc2", n]
                    if kind == "fc2_half":
                        if n == 0:
                            pe.wait_ge(fc2_loaded[0], 16)
                        if n == FC2_FIRST:
                            pe.wait_ge(fc2_loaded[1], 16)
                        pe.wait_ge(s_read, S_RING["fc1", FC * n + FC - 1] + 1)
                        wait_for_bank("m", r)
                    for t in (0, 1) if kind == "fc2_half" else (2, 3):
                        for c in range(FC):
                            mm = nc.tensor.matmul(ps_r[:, bank("m", r), t * D:t * D + D],
                                                  hidden[:, FC * (n % 2) + c, t * P:t * P + P], fc2_sb[:, e, c],
                                                  start=(c == 0), stop=(c == FC - 1))
                    if kind == "fc2":
                        mm.then_inc(m_filled, 1)
                    mm = None
                if mm is not None:
                    mm.then_inc(misc_filled, 1)


def kernel(x, ctx_1024, L0_xattn_sa_ln_g, L0_xattn_sa_ln_b, L0_xattn_sa_in_w, L0_xattn_sa_in_b, L0_xattn_sa_out_w,
           L0_xattn_sa_out_b, L0_xattn_ca_q_ln_g, L0_xattn_ca_q_ln_b, L0_xattn_ca_kv_ln_g, L0_xattn_ca_kv_ln_b,
           L0_xattn_ca_in_w, L0_xattn_ca_in_b, L0_xattn_ca_out_w, L0_xattn_ca_out_b, L0_xattn_moe_ln_g,
           L0_xattn_moe_ln_b, L0_xattn_router_w, L0_xattn_router_b, L0_xattn_e_fc1_w, L0_xattn_e_fc1_b,
           L0_xattn_e_fc2_w, L0_xattn_e_fc2_b):
    import numpy as np
    import concourse.bacc as bacc
    from concourse import mybir as mb
    from concourse.bass_utils import run_bass_kernel_spmd

    def head_minor(a):
        return np.asarray(a).reshape(H, DH, -1).transpose(1, 0, 2).reshape(D, -1)

    def w_in(a):
        a = np.asarray(a)
        return np.concatenate([head_minor(a[0:D]), head_minor(a[D:2 * D]), a[2 * D:]], axis=0).T

    def b_in(a):
        a = np.asarray(a)
        return [head_minor(a[0:D])[:, 0], head_minor(a[D:2 * D])[:, 0], a[2 * D:]]

    cols = np.stack([np.asarray(a) for a in (
        L0_xattn_sa_ln_g, L0_xattn_sa_ln_b, L0_xattn_ca_q_ln_g, L0_xattn_ca_q_ln_b, L0_xattn_ca_kv_ln_g,
        L0_xattn_ca_kv_ln_b, L0_xattn_moe_ln_g, L0_xattn_moe_ln_b, *b_in(L0_xattn_sa_in_b), *b_in(L0_xattn_ca_in_b))]
        + [a for a in np.asarray(L0_xattn_e_fc1_b).reshape(E * FC, P)]
        + [a for a in np.asarray(L0_xattn_router_w)], axis=1)
    rows = np.concatenate([np.asarray(L0_xattn_sa_out_b), np.asarray(L0_xattn_ca_out_b),
                           np.asarray(L0_xattn_router_b)])
    arrays = {
        "x": np.asarray(x),
        "ctx_in": np.asarray(ctx_1024),
        "w_in": np.stack([w_in(L0_xattn_sa_in_w), w_in(L0_xattn_ca_in_w)], axis=1),
        "w_out": np.stack([np.asarray(L0_xattn_sa_out_w).T, np.asarray(L0_xattn_ca_out_w).T], axis=1),
        "cols": cols,
        "rows": rows,
        "fc1_w": np.asarray(L0_xattn_e_fc1_w).transpose(2, 0, 1),
        "fc2_w": np.asarray(L0_xattn_e_fc2_w).reshape(E, D, FC, P).transpose(3, 0, 2, 1),
        "fc2_b": np.asarray(L0_xattn_e_fc2_b),
    }
    arrays = {k: np.ascontiguousarray(a) for k, a in arrays.items()}
    nc = bacc.Bacc("TRN2", target_bir_lowering=False, num_devices=1)
    args = [nc.dram_tensor(k, a.shape, mb.dt.from_np(a.dtype), kind="ExternalInput").ap() for k, a in arrays.items()]
    out = nc.dram_tensor("out", (B, S, D), F32, kind="ExternalOutput").ap()
    build(nc, *args, out)
    result = run_bass_kernel_spmd(nc, [arrays], core_ids=[0])
    return result.results[0]["out"]
```
